# Optimizing a Trainium2 kernel written in Bass

```python
import numpy as np
import jax
import jax.numpy as jnp

def _softmax(x, axis=-1):
    return jax.nn.softmax(x, axis=axis)

def _gelu(x):
    return jax.nn.gelu(x, approximate=True)

def _silu(x):
    return jax.nn.silu(x)

def _sigmoid(x):
    return jax.nn.sigmoid(x)

def _layernorm(x, axis=-1, eps=1e-05):
    m = jnp.mean(x, axis=axis, keepdims=True)
    v = jnp.var(x, axis=axis, keepdims=True)
    return (x - m) / jnp.sqrt(v + eps)

def _scatter_add(tgt, idx, src, axis=0):
    return tgt.at[idx].add(src)

def _segment_sum(src, seg, n):
    return jax.ops.segment_sum(src, seg, n)
kernel_name = 'mk_gnn_resnorm_d2_gnn_r8_558a12'

def setup_inputs(seed: int=0):
    np.random.seed(seed)
    _w = jnp.asarray

    def _rec_inputs():
        import jax
        import jax.numpy as jnp
        _gk = jax.random.key(seed)
        x = -2.02e-05 + 0.1 * jax.random.normal(jax.random.fold_in(_gk, 1), (6250, 64), jnp.float32)
        src = jax.random.randint(jax.random.fold_in(_gk, 2), (200000,), 0, 6250, jnp.int32)
        dst = jnp.minimum((6250 * jax.random.uniform(jax.random.fold_in(_gk, 3), (200000,)) ** 2.0).astype(jnp.int32), 49999)
        _o = jnp.argsort(dst, stable=True)
        src = src[_o]
        dst = dst[_o]
        edge_type_50 = jax.random.randint(jax.random.fold_in(_gk, 12), (200000,), 0, 50, jnp.int32)
        return (x, src, dst, edge_type_50)
    x, src, dst, edge_type_50 = _rec_inputs()

    def _L0_gnn_setup():
        import jax, jax.numpy as jnp
        import numpy as np
        N_HOPS = 2
        LEAKY_SLOPE = 0.2
        EPS = 1e-12
        key = jax.random.key(seed)
        k1, k2, k3, k4, k5, k6 = jax.random.split(key, 6)
        N, R, C, E = (12500, 50, 64, 125000)
        return {'entity_emb': jax.random.normal(k1, (N, C), dtype=jnp.float32) * 0.1, 'relation_emb': jax.random.normal(k2, (R, C), dtype=jnp.float32) * 0.1, 'fc_w': jax.random.normal(k3, (C, 2 * C), dtype=jnp.float32) * 0.1, 'fc_b': jax.random.normal(k4, (C,), dtype=jnp.float32) * 0.1, 'edge_index': jax.random.randint(k5, (2, E), 0, N, dtype=jnp.int64), 'edge_type': jax.random.randint(k6, (E,), 0, R, dtype=jnp.int64)}
    _L0_gnn_all = _L0_gnn_setup()
    _L0_gnn_in = {k: v for k, v in _L0_gnn_all.items() if k in ('relation_emb', 'fc_w', 'fc_b')}
    del _L0_gnn_all

    def _L1_gnn_setup():
        import jax, jax.numpy as jnp
        import numpy as np
        N_NODES = 12500
        N_EDGES = 200000
        IN_DIM = 64
        OUT_DIM = 64
        FLAT = IN_DIM * OUT_DIM

        def _gru_cell(inp, hid, w_ih, w_hh, b_ih, b_hh):
            gi = w_ih @ inp + b_ih
            gh = w_hh @ hid + b_hh
            i_r, i_z, i_n = jnp.split(gi, 3)
            h_r, h_z, h_n = jnp.split(gh, 3)
            r = jax.nn.sigmoid(i_r + h_r)
            z = jax.nn.sigmoid(i_z + h_z)
            n = jnp.tanh(i_n + r * h_n)
            return (1.0 - z) * n + z * hid
        key = jax.random.key(seed)
        ks = jax.random.split(key, 8)
        x = jax.random.normal(ks[0], (N_NODES, IN_DIM), dtype=jnp.float32)
        row = jax.random.randint(ks[1], (N_EDGES,), 0, N_NODES)
        offs = jax.random.randint(ks[2], (N_EDGES,), 1, N_NODES)
        col = (row + offs) % N_NODES
        edge_index = jnp.stack([row, col]).astype(jnp.int64)
        limit = float(np.sqrt(6.0 / (IN_DIM + OUT_DIM)))
        initial_weight = jax.random.uniform(ks[3], (IN_DIM, OUT_DIM), jnp.float32, -limit, limit)
        s = 1.0 / np.sqrt(FLAT)
        w_ih = jax.random.uniform(ks[4], (3 * FLAT, FLAT), jnp.float32, -s, s)
        w_hh = jax.random.uniform(ks[5], (3 * FLAT, FLAT), jnp.float32, -s, s)
        b_ih = jax.random.uniform(ks[6], (3 * FLAT,), jnp.float32, -s, s)
        b_hh = jax.random.uniform(ks[7], (3 * FLAT,), jnp.float32, -s, s)
        return {'x': x, 'edge_index': edge_index, 'initial_weight': initial_weight, 'w_ih': w_ih, 'w_hh': w_hh, 'b_ih': b_ih, 'b_hh': b_hh}
    _L1_gnn_all = _L1_gnn_setup()
    _L1_gnn_in = {k: v for k, v in _L1_gnn_all.items() if k in ('initial_weight', 'w_ih', 'w_hh', 'b_ih', 'b_hh')}
    del _L1_gnn_all
    return {'x': x, 'src': src, 'dst': dst, 'edge_type_50': edge_type_50, 'L0_gnn_relation_emb': _L0_gnn_in['relation_emb'], 'L0_gnn_fc_w': _L0_gnn_in['fc_w'], 'L0_gnn_fc_b': _L0_gnn_in['fc_b'], 'L1_gnn_initial_weight': _L1_gnn_in['initial_weight'], 'L1_gnn_w_ih': _L1_gnn_in['w_ih'], 'L1_gnn_w_hh': _L1_gnn_in['w_hh'], 'L1_gnn_b_ih': _L1_gnn_in['b_ih'], 'L1_gnn_b_hh': _L1_gnn_in['b_hh']}

def reference(x, src, dst, edge_type_50, L0_gnn_relation_emb, L0_gnn_fc_w, L0_gnn_fc_b, L1_gnn_initial_weight, L1_gnn_w_ih, L1_gnn_w_hh, L1_gnn_b_ih, L1_gnn_b_hh):
    import jax
    import jax.numpy as jnp

    def _L0_gnn_ref(entity_emb, relation_emb, fc_w, fc_b, edge_index, edge_type):
        import jax, jax.numpy as jnp
        import numpy as np
        N_HOPS = 2
        LEAKY_SLOPE = 0.2
        EPS = 1e-12
        'RGAT.forward with mess_dropout=False: n_hops of relational-attention\n            gather -> leakyrelu -> scatter_softmax(head) -> scatter_sum -> residual -> L2 normalize.'
        N = entity_emb.shape[0]
        head, tail = (edge_index[0], edge_index[1])
        rel_e = relation_emb[edge_type]

        def agg(emb):
            a_input = jnp.concatenate([emb[head], emb[tail]], axis=-1)
            h = a_input @ fc_w.T + fc_b
            e = jnp.sum(h * rel_e, axis=-1)
            e = jnp.where(e > 0, e, LEAKY_SLOPE * e)
            m = jax.ops.segment_max(e, head, num_segments=N)
            ex = jnp.exp(e - m[head])
            denom = jax.ops.segment_sum(ex, head, num_segments=N)
            w = ex / denom[head]
            agg_emb = jax.ops.segment_sum(emb[tail] * w[:, None], head, num_segments=N)
            agg_emb = agg_emb + emb
            return agg_emb
        emb = entity_emb
        for _ in range(N_HOPS):
            emb = agg(emb)
            nrm = jnp.sqrt(jnp.sum(emb * emb, axis=-1, keepdims=True))
            emb = emb / jnp.maximum(nrm, EPS)
        return emb

    def _L1_gnn_ref(x, edge_index, initial_weight, w_ih, w_hh, b_ih, b_hh):
        import jax, jax.numpy as jnp
        import numpy as np
        N_NODES = 12500
        N_EDGES = 200000
        IN_DIM = 64
        OUT_DIM = 64
        FLAT = IN_DIM * OUT_DIM

        def _gru_cell(inp, hid, w_ih, w_hh, b_ih, b_hh):
            gi = w_ih @ inp + b_ih
            gh = w_hh @ hid + b_hh
            i_r, i_z, i_n = jnp.split(gi, 3)
            h_r, h_z, h_n = jnp.split(gh, 3)
            r = jax.nn.sigmoid(i_r + h_r)
            z = jax.nn.sigmoid(i_z + h_z)
            n = jnp.tanh(i_n + r * h_n)
            return (1.0 - z) * n + z * hid
        num_nodes = x.shape[0]
        in_dim, out_dim = initial_weight.shape
        h = initial_weight.reshape(-1)
        weight = _gru_cell(h, h, w_ih, w_hh, b_ih, b_hh).reshape(in_dim, out_dim)
        loop = jnp.arange(num_nodes, dtype=edge_index.dtype)
        row = jnp.concatenate([edge_index[0], loop])
        col = jnp.concatenate([edge_index[1], loop])
        deg = jax.ops.segment_sum(jnp.ones_like(col, dtype=x.dtype), col, num_segments=num_nodes)
        dis = jnp.where(deg > 0, jax.lax.rsqrt(jnp.maximum(deg, 1.0)), 0.0)
        norm = dis[row] * dis[col]
        xw = x @ weight
        msg = xw[row] * norm[:, None]
        out = jax.ops.segment_sum(msg, col, num_segments=num_nodes)
        return jax.nn.relu(out)
    edge_index = jnp.stack([src, dst])
    x = _layernorm(x + _L0_gnn_ref(x, L0_gnn_relation_emb, L0_gnn_fc_w, L0_gnn_fc_b, edge_index, edge_type_50), axis=-1)
    x = _layernorm(x + _L1_gnn_ref(x, edge_index, L1_gnn_initial_weight, L1_gnn_w_ih, L1_gnn_w_hh, L1_gnn_b_ih, L1_gnn_b_hh), axis=-1)
    return x

_drawn_inputs = setup_inputs


def setup_inputs(seed=0):
    import zlib

    import numpy as np

    out = dict(_drawn_inputs(seed))
    spreads = {}
    factors = {'L0_gnn_relation_emb': 3.461,
     'L0_gnn_fc_w': 4.466,
     'L0_gnn_fc_b': 5.629,
     'L1_gnn_w_hh': 2.704,
     'L1_gnn_b_ih': 8.0,
     'L1_gnn_b_hh': 8.0}
    for name, (base, spread) in spreads.items():
        noise = np.random.default_rng([zlib.crc32(name.encode()), seed]).standard_normal(out[name].shape)
        drawn = base * np.exp(spread * noise) if base else spread * noise
        out[name] = jnp.asarray(drawn.astype(out[name].dtype))
    for name, factor in factors.items():
        out[name] = (out[name] * factor).astype(out[name].dtype)
    return out
```

```python
from contextlib import ExitStack

import concourse.bass as bass
from concourse import mybir

ALU = mybir.AluOpType
ACT = mybir.ActivationFunctionType
AX = mybir.AxisListType.X
F32 = mybir.dt.float32
BF16 = mybir.dt.bfloat16
I32 = mybir.dt.int32

P = 128
BIG = float(2.0 ** 100)
NO_SCORE = -float(2.0 ** 97)
PAD_DST = 30000
PAD_LO = 200
KT = 4
GE = KT * P


def ds(start, n):
    return bass.ds(start, n)


def loop(eng, lo, hi, step=1):
    return eng.bass.Fori(lo, hi, step, engines=(eng.engine,), hint_back_edge=True)


def wait(eng, sem, value):
    if isinstance(value, int) and value <= 0:
        return
    eng.wait_ge(sem, value)


def wait_pool(pool, tick, sem, value):
    if isinstance(value, int) and value <= 0:
        return
    pool.wait_ge(sem, value)
    pool.sem_inc(tick, 1)


class Chain:

    def __init__(self, eng, sem, tick=None):
        self.eng, self.sem, self.tick, self.base, self.n = eng, sem, tick, 0, 0

    def __call__(self, ins):
        self.n += 1
        ins.then_inc(self.sem, 1)
        self.eng.wait_ge(self.sem, self.base + self.n)

    def mark(self, ins):
        self.n += 1
        ins.then_inc(self.sem, 1)

    def sync(self):
        self.eng.wait_ge(self.sem, self.base + self.n)

    def loop(self, lo, hi, per, body):
        before = self.base + self.n
        with loop(self.eng, lo, hi) as i:
            self.base, self.n = (i - lo) * per + before if lo else i * per + before, 0
            body(i)
            self.eng.sem_inc(self.tick, 1)
            assert self.n == per, (self.n, per)
        self.base, self.n = before + (hi - lo) * per, 0


def pipelined(eng, n, lag, unroll, body):
    assert n % unroll == 0 and lag <= unroll
    for i in range(unroll):
        body(i, i)
    with loop(eng, unroll, n - unroll + 1, unroll) as i0:
        for u in range(unroll):
            body(i0 + u, u)
    for i in range(n, n + lag):
        body(i, i % unroll)


def pipelined_counted(eng, link, n, lag, unroll, body):
    def span(lo, step):
        start = link.base + link.n
        for u in range(unroll):
            body(lo + u, u)
        return link.base + link.n - start

    span(0, 1)
    before = link.base + link.n
    with loop(eng, unroll, n - unroll + 1, unroll) as i0:
        link.base, link.n = (i0 - unroll) * PER_GROUP + before, 0
        for u in range(unroll):
            body(i0 + u, u)
        assert link.n == PER_GROUP * unroll, link.n
    link.base, link.n = before + (n - unroll) * PER_GROUP, 0
    for i in range(n, n + lag):
        body(i, i % unroll)


PER_GROUP = 10


def stages(i, n):
    if not isinstance(i, int):
        return True, True, True, True
    return i < n, 1 <= i <= n, 2 <= i <= n + 1, i >= 3


def gnn_kernel(nc, x, src, dst, typ, relT, fc_w, fc_b, w_ih, w_hh, h_col, h_mat, b_ih, b_hh, out):
    N, C = x.shape
    E = src.shape[0]
    R = relT.shape[1]
    NB = -(-N // P)
    FULL, REST = N // P, N % P
    PS = 125
    ES = E // PS
    assert PS * ES == E and ES % 32 == 0
    NG0 = -(-(E + NB * (GE - 1)) // GE)
    NG = -(-NG0 // 8) * 8
    T1 = NG * KT
    NGD = -(-(-(-E // GE)) // 8) * 8
    GP = NGD // 4
    GLAST = E // GE
    TD = NGD * KT
    W = 128
    ONE, SC = C, C + 1
    FLAT = C * C
    KC = FLAT // P
    RC = 3 * FLAT // 512
    PC = KC // 4
    RING = 4
    AB = 2 * NB + 2

    with ExitStack() as ctx:
        def sb(name, shape, dt=F32):
            return ctx.enter_context(nc.sbuf_tensor(name, shape, dt))

        def sem(name):
            return ctx.enter_context(nc.semaphore(name))

        rec_d = nc.dram_tensor("rec_d", (P * T1, 4), I32).ap()
        tab_d = [nc.dram_tensor(f"tab{h}_d", (NB * P, W), F32).ap() for h in range(2)]
        y_d = nc.dram_tensor("y_d", (NB * P, C), F32).ap()
        gate_d = nc.dram_tensor("gate_d", (2 * RC, 512), F32).ap()

        iota_f = sb("iota_f", [P, 512])
        iota_b = sb("iota_b", [P, 256], BF16)
        ident_f = sb("ident_f", [P, P])
        ident_b = sb("ident_b", [P, P], BF16)
        x0 = sb("x0", [P, NB, C])
        p12 = sb("p12", [P, 2 * R])
        group_block = sb("group_block", [P, NG], I32)
        window0 = sb("window0", [P, NGD], I32)
        n_sweeps = sb("n_sweeps", [P, 1], I32)
        rel_dst = sb("rel_dst", [P, NGD, KT])
        src_cols = sb("src_cols", [P, NGD, KT], I32)
        dis = sb("dis", [P, NB])
        weight = sb("weight", [P, C])
        const_rdy = sem("const_rdy")

        with ExitStack() as ph:
            def sb1(name, shape, dt=F32):
                return ph.enter_context(nc.sbuf_tensor(name, shape, dt))

            def ps1(name, shape, dt=F32):
                return ph.enter_context(nc.psum_tensor(name, shape, dt))

            def sem1(name):
                return ph.enter_context(nc.semaphore(name))

            iota_i = sb1("iota_i", [P, 512], I32)
            part_i = sb1("part_i", [P, 1], I32)
            part_f = sb1("part_f", [P, 1])
            tri = sb1("tri", [P, P])
            ones = sb1("ones", [P, P])
            idx_i = sb1("idx_i", [PS, 3, ES], I32)
            blk_b = sb1("blk_b", [PS, ES], BF16)
            rec = sb1("rec", [PS, ES, 4], I32)
            one_b = sb1("one_b", [PS, ES], BF16)
            mask_b = sb1("mask_b", [PS, ES], BF16)
            buf_a = sb1("buf_a", [P, max(ES, TD)])
            buf_b = sb1("buf_b", [P, max(ES, TD)])
            cum, pos = buf_a[0:PS, 0:ES], buf_b[0:PS, 0:ES]
            row = sb1("row", [PS, ES], I32)
            counts = sb1("counts", [PS, NB])
            base = sb1("base", [PS, NB])
            tot = sb1("tot", [P, NB])
            n_groups_i = sb1("n_groups_i", [P, NB], I32)
            n_groups = sb1("n_groups", [P, NB])
            end_group = sb1("end_group", [P, NB])
            gb = sb1("gb", [P, NG])
            blank = sb1("blank", [P, 32, 4], I32)
            stage_row = sb1("stage_row", [PS, 2, 16], I32)
            stage_rec = sb1("stage_rec", [PS, 2, 16, 4], I32)
            grp_dst = sb1("grp_dst", [GP, 4, GE], I32)
            grp_src = sb1("grp_src", [GP, 4, GE], I32)
            grp_f = sb1("grp_f", [GP, 4, GE])
            grp_hi = sb1("grp_hi", [GP, 4, GE])
            lowest = sb1("lowest", [GP, 4])
            highest = sb1("highest", [GP, 4])
            span = sb1("span", [GP, 1])
            dst_t = sb1("dst_t", [P, NGD, KT])
            dst_ti = sb1("dst_ti", [P, NGD, KT], I32)
            lo_t, hi_t = buf_a[:, 0:TD], buf_b[:, 0:TD]
            win_f = sb1("win_f", [P, NGD])
            sw_f = sb1("sw_f", [P, 1])
            deg = sb1("deg", [P, NB])
            lo_hot = sb1("lo_hot", [P, 8, P], BF16)
            hi_hot = sb1("hi_hot", [P, 8, 64], BF16)
            h_sb = sb1("h_sb", [P, KC])
            ring = sb1("ring", [P, RING, 4, 512])
            gate_row = sb1("gate_row", [1, 2, 512])

            ps_small = ps1("ps_small", [P, 2, 256])
            ps_t = ps1("ps_t", [P, 2, 512])
            ps_gate = ps1("ps_gate", [1, 2, 512])
            ps_deg = ps1("ps_deg", [P, 512])

            iota_rdy, idx_ld, grp_ld, h_ld, x_ld = map(sem1, ("iota_rdy", "idx_ld", "grp_ld", "h_ld", "x_ld"))
            dv, blank_rdy, blank_st, grp_set = map(sem1, ("dv", "blank_rdy", "blank_st", "grp_set"))
            cnt_rdy, pre_rdy, row_rdy, rec_rdy = map(sem1, ("cnt_rdy", "pre_rdy", "row_rdy", "rec_rdy"))
            grp_rdy, tp_rdy, tp_used, lim_rdy, lim_t = map(sem1, ("grp_rdy", "tp_rdy", "tp_used", "lim_rdy", "lim_t"))
            staged, tick = sem1("staged"), sem1("tick")
            scattered = [sem1(f"scattered{h}") for h in range(2)]
            piece_ld = [sem1(f"piece_ld{i}") for i in range(RING)]
            piece_used, gate_cp = sem1("piece_used"), sem1("gate_cp")
            gate_st = [sem1(f"gate_st{i}") for i in range(2)]
            dtick1 = sem1("dtick1")
            hot_rdy, hot_used = sem1("hot_rdy"), sem1("hot_used")

            block = ph.enter_context(nc.Block())

            @block.sync
            def _(sp):
                for i, v in enumerate((src, dst, typ)):
                    sp.dma_start(idx_i[:, i, :], v.rearrange("(p t) -> p t", p=PS)).then_inc(idx_ld, 16)
                sp.wait_ge(grp_set, 2)
                for v, t in ((dst, grp_dst), (src, grp_src)):
                    for c in range(4):
                        n = min(GP, GLAST - c * GP)
                        sp.dma_start(t[0:n, c, :], v[c * GP * GE:(c * GP + n) * GE].rearrange("(p e) -> p e", e=GE)
                                     ).then_inc(grp_ld, 16)
                    n = E - GLAST * GE
                    sp.dma_start(t[GLAST - 3 * GP:GLAST - 3 * GP + 1, 3, 0:n],
                                 v[GLAST * GE:E].rearrange("(p e) -> p e", p=1)).then_inc(grp_ld, 16)
                sp.dma_start(h_sb[:], h_col).then_inc(h_ld, 16)
                for m, w in enumerate((w_ih, w_hh)):
                    def pieces(n):
                        for pc in range(PC):
                            wait(sp, piece_used, (m * RC + n) * PC + pc - RING + 1)
                            sp.dma_start(ring[:, pc % RING].rearrange("p q c -> p (q c)"),
                                         w[ds(n, 1), pc].rearrange("a p q c -> (a p) (q c)")).then_inc(piece_ld[pc % RING], 16)
                    if m == 0:
                        pieces(0)
                    with loop(sp, 1 - m, RC) as n:
                        pieces(n)

            @block.gpsimd
            def _(pool):
                pool.iota(iota_i[:], pattern=[[1, 512]], base=0, channel_multiplier=0).then_inc(iota_rdy, 1)
                pool.iota(part_i[:], pattern=[[0, 1]], base=0, channel_multiplier=1).then_inc(iota_rdy, 1)
                pool.memset(grp_dst[:], PAD_DST).then_inc(grp_set, 1)
                pool.memset(grp_src[:], 0).then_inc(grp_set, 1)

                def batch(b, h, first):
                    if not first:
                        wait_pool(pool, tick, scattered[h], b * 256)
                    t0 = b * 32 + h * 16
                    pool.tensor_copy(stage_row[:, h, :], row[:, ds(t0, 16)]).then_inc(staged, 1)
                    pool.tensor_copy(stage_rec[:, h], rec[:, ds(t0, 16), :]).then_inc(staged, 1)
                    wait_pool(pool, tick, staged, b * 4 + h * 2 + 2)
                    for j in range(16):
                        pool.indirect_dma_start(
                            out=rec_d, out_offset=bass.IndirectOffsetOnAxis(ap=stage_row[:, h, j:j + 1], axis=0),
                            in_=stage_rec[:, h, j, :], in_offset=None).then_inc(scattered[h], 16)

                pool.wait_ge(row_rdy, 1)
                pool.wait_ge(rec_rdy, 3)
                pool.wait_ge(blank_st, 16)
                for h in range(2):
                    batch(0, h, True)
                with loop(pool, 1, ES // 32) as b:
                    for h in range(2):
                        batch(b, h, False)
                for h in range(2):
                    pool.wait_ge(scattered[h], ES // 32 * 256)

            @block.scalar
            def _(act):
                act.wait_ge(blank_rdy, 2)
                act.dma_start(rec_d.rearrange("(p t) f -> p t f", p=P).rearrange("p (a b) f -> p a (b f)", b=32),
                              blank[:].rearrange("p b f -> p (b f)").unsqueeze(1).broadcast_to([P, T1 // 32, 128])
                              ).then_inc(blank_st, 16)
                act.wait_ge(x_ld, 1)
                act.dma_start(x0[:, 0:FULL, :], x[0:FULL * P].rearrange("(b p) c -> p b c", p=P)).then_inc(x_ld, 16)
                act.dma_start(x0[0:REST, FULL, :], x[FULL * P:N]).then_inc(x_ld, 16)
                act.wait_ge(idx_ld, 48)
                act.activation(rec[:, :, 1], idx_i[:, 1, :], ACT.Copy).then_inc(rec_rdy, 1)
                act.activation(rec[:, :, 2], idx_i[:, 2, :], ACT.Copy).then_inc(rec_rdy, 1)

                def evacuate(k, s):
                    act.wait_ge(piece_used, (k + 1) * PC)
                    act.activation(gate_row[:, s, :], ps_gate[:, s, :], ACT.Copy).then_inc(gate_cp, 1)
                    act.wait_ge(gate_cp, k + 1)
                    act.dma_start(gate_d[ds(k, 1), :], gate_row[:, s, :]).then_inc(gate_st[s], 16)

                for s in range(2):
                    evacuate(s, s)
                with loop(act, 1, RC) as k2:
                    for s in range(2):
                        act.wait_ge(gate_st[s], k2 * 16)
                        evacuate(k2 * 2 + s, s)
                for s in range(2):
                    act.wait_ge(gate_st[s], RC * 16)
                act.wait_ge(x_ld, 33)

            @block.tensor
            def _(pe):
                pe.wait_ge(const_rdy, 1)
                for i in range(2 * 4 * KT):
                    v, c, k = i // (4 * KT), i // KT % 4, i % KT
                    pe.wait_ge(grp_rdy, v + 1)
                    wait(pe, tp_used, i - 1)
                    pe.transpose(ps_t[:, i % 2, 0:GP], grp_f[:, c, k * P:(k + 1) * P] if v == 0 else
                                 grp_hi[:, c, k * P:(k + 1) * P], ident_f[0:GP, 0:GP]).then_inc(tp_rdy, 1)
                pe.wait_ge(cnt_rdy, 1)
                pe.wait_ge(tp_used, 2 * 4 * KT)
                pe.matmul(ps_small[0:PS, 0, 0:NB], lhsT=tri[0:PS, 0:PS], rhs=counts[:], start=True, stop=True)
                pe.matmul(ps_small[:, 1, 0:NB], lhsT=ones[0:PS, :], rhs=counts[:], start=True, stop=True
                          ).then_inc(pre_rdy, 1)
                pe.wait_ge(h_ld, 16)

                def chunk(k, s):
                    for pc in range(PC):
                        pe.wait_ge(piece_ld[pc % RING], k * (PC // RING * 16) + (pc // RING + 1) * 16)
                        if pc == 0:
                            wait(pe, gate_cp, k - 1)
                        for q in range(4):
                            kc = pc * 4 + q
                            mm = pe.matmul(ps_gate[:, s, :], lhsT=h_sb[:, kc:kc + 1], rhs=ring[:, pc % RING, q, :],
                                           start=(kc == 0), stop=(kc == KC - 1))
                        mm.then_inc(piece_used, 1)

                for s in range(2):
                    chunk(s, s)
                with loop(pe, 2, 2 * RC - 1, 2) as k0:
                    for s in range(2):
                        chunk(k0 + s, s)
                pe.wait_ge(lim_rdy, 1)
                for c in range(4):
                    pe.transpose(ps_t[:, 0, c * GP:(c + 1) * GP], lowest[:, c:c + 1].broadcast_to([GP, P]),
                                 ident_f[0:GP, 0:GP])
                pe.transpose(ps_t[:, 1, 0:GP], span[:].broadcast_to([GP, P]), ident_f[0:GP, 0:GP]).then_inc(lim_t, 1)
                def count(i, j, first=False, last=False):
                    pe.matmul(ps_deg[:, 0:NB], lhsT=lo_hot[:, j, :], rhs=hi_hot[:, j, 0:NB], start=first,
                              stop=last, skip_group_check=True).then_inc(hot_used, 1)
                pe.wait_ge(hot_rdy, 1)
                for j in range(8):
                    pe.wait_ge(hot_rdy, j + 1)
                    count(0, j, first=(j == 0))
                with loop(pe, 8, TD - 15, 8) as t0:
                    for j in range(8):
                        pe.wait_ge(hot_rdy, t0 + j + 1)
                        count(t0, j)
                for j in range(8):
                    pe.wait_ge(hot_rdy, TD - 8 + j + 1)
                    count(0, j, last=(j == 7))

            @block.vector
            def _(dve):
                link = Chain(dve, dv, dtick1)
                dve.memset(ones[:], 1.0)
                dve.memset(one_b[:], 1.0)
                dve.memset(pos, 0.0)
                dve.memset(gb[:], 0.0)
                link.mark(dve.memset(blank[:], 0))
                link.sync()
                dve.memset(blank[:, :, 0], PAD_LO).then_inc(blank_rdy, 2)
                dve.memset(x0[:], 0.0).then_inc(x_ld, 1)
                link(dve.memset(rec[:, :, 3], 0))
                dve.wait_ge(iota_rdy, 2)
                dve.tensor_copy(iota_b[:], iota_i[:, 0:256])
                dve.tensor_copy(iota_f[:], iota_i[:])
                link(dve.tensor_copy(part_f[:], part_i[:]))
                link.mark(dve.tensor_scalar(ident_f[:], iota_f[:, 0:P], part_f[:], None, ALU.is_equal))
                link.mark(dve.tensor_scalar(ident_b[:], iota_f[:, 0:P], part_f[:], None, ALU.is_equal))
                link(dve.tensor_scalar(tri[:], iota_f[:, 0:P], part_f[:], None, ALU.is_gt))
                dve.sem_inc(const_rdy, 1)
                dve.wait_ge(idx_ld, 48)
                link(dve.tensor_scalar(row[:], idx_i[:, 0, :], 7, None, ALU.logical_shift_right))
                link(dve.tensor_copy(blk_b[:], row[:]))
                link(dve.tensor_scalar(row[:], idx_i[:, 0, :], P - 1, None, ALU.bitwise_and))
                dve.tensor_copy(rec[:, :, 0], row[:]).then_inc(rec_rdy, 1)
                def count(b):
                    link(dve.scalar_tensor_tensor(out=mask_b[:], in0=blk_b[:], scalar=iota_f[0:PS, ds(b, 1)],
                                                  in1=one_b[:], op0=ALU.is_equal, op1=ALU.mult,
                                                  accum_out=counts[:, ds(b, 1)]))
                link.loop(0, NB, 1, count)
                dve.sem_inc(cnt_rdy, 1)
                dve.wait_ge(grp_ld, 160)
                link(dve.tensor_copy(grp_f[:], grp_dst[:]))
                dve.sem_inc(grp_rdy, 1)
                link(dve.tensor_copy(grp_hi[:], grp_src[:]))
                dve.sem_inc(grp_rdy, 1)
                for i in range(2 * 4 * KT):
                    v, c, k = i // (4 * KT), i // KT % 4, i % KT
                    dve.wait_ge(tp_rdy, i + 1)
                    to = (dst_t, src_cols)[v]
                    dve.tensor_copy(to[:, c * GP:(c + 1) * GP, k], ps_t[:, i % 2, 0:GP]).then_inc(tp_used, 1)
                dve.wait_ge(pre_rdy, 1)
                link(dve.tensor_scalar(tot[:], ps_small[:, 1, 0:NB], float(GE - 1), None, ALU.add))
                link(dve.tensor_copy(n_groups_i[:], tot[:]))
                link(dve.tensor_scalar(n_groups_i[:], n_groups_i[:], 9, None, ALU.logical_shift_right))
                link(dve.tensor_copy(n_groups[:], n_groups_i[:]))
                link(dve.tensor_tensor_scan(end_group[:], ones[:, 0:NB], n_groups[:], 0.0, ALU.mult, ALU.add))
                link(dve.tensor_tensor(base[:], end_group[0:PS], n_groups[0:PS], ALU.subtract))
                link(dve.scalar_tensor_tensor(out=base[:], in0=base[:], scalar=float(GE), in1=ps_small[0:PS, 0, 0:NB],
                                              op0=ALU.mult, op1=ALU.add))
                def place(b):
                    link(dve.tensor_scalar(mask_b[:], blk_b[:], iota_f[0:PS, ds(b, 1)], None, ALU.is_equal))
                    link(dve.tensor_tensor_scan(cum, one_b[:], mask_b[:], base[:, ds(b, 1)], ALU.mult, ALU.add))
                    link(dve.tensor_tensor(cum, cum, mask_b[:], ALU.mult))
                    link(dve.tensor_tensor(pos, pos, cum, ALU.add))
                link.loop(0, NB, 4, place)
                link(dve.tensor_scalar(row[:], pos, -1.0, None, ALU.add))
                dve.wait_ge(rec_rdy, 3)
                link.mark(dve.tensor_scalar(idx_i[:, 0, :], row[:], P - 1, None, ALU.bitwise_and))
                link(dve.tensor_scalar(idx_i[:, 1, :], row[:], 7, None, ALU.logical_shift_right))
                dve.scalar_tensor_tensor(out=row[:], in0=idx_i[:, 0, :], scalar=float(T1), in1=idx_i[:, 1, :],
                                         op0=ALU.mult, op1=ALU.add).then_inc(row_rdy, 1)
                def group(b):
                    link(dve.scalar_tensor_tensor(out=gb[:], in0=iota_f[:, 0:NG], scalar=end_group[:, ds(b, 1)],
                                                  in1=gb[:], op0=ALU.is_ge, op1=ALU.add))
                link.loop(0, NB, 1, group)
                link(dve.tensor_scalar(group_block[:], gb[:], float(NB - 1), None, ALU.min))
                link(dve.tensor_scalar(grp_dst[:], grp_dst[:], 7, None, ALU.logical_shift_right))
                link(dve.tensor_copy(grp_hi[:], grp_dst[:]))
                link(dve.tensor_reduce(lowest[:], grp_hi[:], AX, ALU.min))
                link(dve.scalar_tensor_tensor(out=grp_f[:], in0=grp_hi[:], scalar=float(NB), in1=grp_hi[:],
                                              op0=ALU.is_lt, op1=ALU.mult))
                link(dve.tensor_reduce(highest[:], grp_f[:], AX, ALU.max))
                link(dve.tensor_scalar(lowest[:], lowest[:], float(NB - 1), None, ALU.min))
                link(dve.tensor_tensor(highest[:], highest[:], lowest[:], ALU.subtract))
                link(dve.tensor_reduce(span[:], highest[:], AX, ALU.max))
                dve.sem_inc(lim_rdy, 1)
                link(dve.tensor_copy(dst_ti[:], dst_t[:]))
                link.mark(dve.tensor_scalar(rel_dst[:].bitcast(I32), dst_ti[:], P - 1, None, ALU.bitwise_and))
                link(dve.tensor_scalar(dst_ti[:], dst_ti[:], 7, None, ALU.logical_shift_right))
                link.mark(dve.tensor_copy(lo_t, rel_dst[:].bitcast(I32).rearrange("p g k -> p (g k)")))
                link(dve.tensor_copy(hi_t, dst_ti[:].rearrange("p g k -> p (g k)")))

                def hots(t, j):
                    wait(dve, hot_used, t - 7)
                    dve.tensor_scalar(lo_hot[:, j, :], iota_b[:, 0:P], lo_t[:, ds(t, 1)], None, ALU.is_equal)
                    dve.tensor_scalar(hi_hot[:, j, :], iota_b[:, 0:64], hi_t[:, ds(t, 1)], None, ALU.is_equal
                                      ).then_inc(hot_rdy, 1)
                for j in range(8):
                    hots(j, j)
                with loop(dve, 8, TD - 7, 8) as t0:
                    for j in range(8):
                        hots(t0 + j, j)
                dve.wait_ge(lim_t, 1)
                link.mark(dve.tensor_copy(win_f[:], ps_t[:, 0, 0:NGD]))
                link.mark(dve.tensor_copy(window0[:], ps_t[:, 0, 0:NGD]))
                link(dve.tensor_reduce(sw_f[:], ps_t[:, 1, 0:GP], AX, ALU.max))
                link(dve.tensor_copy(n_sweeps[:], sw_f[:]))
                link(dve.tensor_scalar(n_sweeps[:], n_sweeps[:], 1, None, ALU.logical_shift_right))
                link(dve.tensor_copy(sw_f[:], n_sweeps[:]))
                link(dve.tensor_scalar(n_sweeps[:], sw_f[:], 1.0, None, ALU.add))
                link(dve.scalar_tensor_tensor(out=rel_dst[:], in0=win_f[:].unsqueeze(2).broadcast_to([P, NGD, KT]),
                                              scalar=-float(P), in1=dst_t[:], op0=ALU.mult, op1=ALU.add))
                dve.wait_ge(hot_used, TD)
                link(dve.tensor_scalar(deg[:], ps_deg[:, 0:NB], 1.0, None, ALU.add))
                link(dve.tensor_copy(dis[:], deg[:]))

        tab = sb("tab", [P, NB, W])
        lo_e = sb("lo_e", [P, T1])
        typ_e = sb("typ_e", [P, T1])
        dst_e = sb("dst_e", [P, T1], I32)

        with ExitStack() as ph:
            def sb2(name, shape, dt=F32):
                return ph.enter_context(nc.sbuf_tensor(name, shape, dt))

            def sem2(name):
                return ph.enter_context(nc.semaphore(name))

            g_sb = sb2("g_sb", [C, 2, 3, C])
            b_sb = sb2("b_sb", [C, 2, 3, C])
            h0 = sb2("h0", [C, C])
            rz = sb2("rz", [C, 2, C])
            nn = sb2("nn", [C, C])
            tmp = sb2("tmp", [C, C])
            fcw = sb2("fcw", [C, 2 * C])
            fcb = sb2("fcb", [C, 1])
            rel = sb2("rel", [C, R])
            rec_e = sb2("rec_e", [P, T1, 4], I32)
            ps_p = ph.enter_context(nc.psum_tensor("ps_p", [P, 3, 128], F32))
            rec_ld = sem2("rec_ld")
            ld2, fc_ld, dv2, s_rdy, rz_rdy, n_rdy, t_rdy, p_rdy, sq_rdy = map(
                sem2, ("ld2", "fc_ld", "dv2", "s_rdy", "rz_rdy", "n_rdy", "t_rdy", "p_rdy", "sq_rdy"))
            block = ph.enter_context(nc.Block())

            @block.sync
            def _(sp):
                sp.dma_start(rec_e[:].rearrange("p t f -> p (t f)"), rec_d.rearrange("(p t) f -> p (t f)", p=P)
                             ).then_inc(rec_ld, 16)
                sp.dma_start(fcw[:], fc_w).then_inc(fc_ld, 16)
                sp.dma_start(fcb[:], fc_b).then_inc(fc_ld, 16)
                sp.dma_start(rel[:], relT).then_inc(fc_ld, 16)
                gv = gate_d.rearrange("(m k) c -> m (k c)", m=2).rearrange("m (t i o) -> m t i o", t=3, o=C)
                for m, b in enumerate((b_ih, b_hh)):
                    for t in range(3):
                        sp.dma_start(g_sb[:, m, t, :], gv[m, t]).then_inc(ld2, 16)
                    sp.dma_start(b_sb[:, m], b.rearrange("(t i o) -> i t o", t=3, o=C)).then_inc(ld2, 16)
                sp.dma_start(h0[:], h_mat).then_inc(ld2, 16)

            @block.tensor
            def _(pe):
                pe.wait_ge(fc_ld, 48)
                pe.matmul(ps_p[0:C, 0, 0:R], lhsT=fcw[:, 0:C], rhs=rel[:], start=True, stop=True)
                pe.matmul(ps_p[0:C, 1, 0:R], lhsT=fcw[:, C:2 * C], rhs=rel[:], start=True, stop=True)
                pe.matmul(ps_p[C:C + 1, 2, 0:R], lhsT=fcb[:], rhs=rel[:], start=True, stop=True).then_inc(p_rdy, 1)

            @block.vector
            def _(dve):
                link = Chain(dve, dv2)
                dve.wait_ge(p_rdy, 1)
                link(dve.memset(p12[:], 0.0))
                link.mark(dve.tensor_copy(p12[0:C, 0:R], ps_p[0:C, 0, 0:R]))
                link.mark(dve.tensor_copy(p12[0:C, R:2 * R], ps_p[0:C, 1, 0:R]))
                link.mark(dve.tensor_copy(p12[C:C + 1, R:2 * R], ps_p[C:C + 1, 2, 0:R]))
                dve.wait_ge(sq_rdy, 1)
                link(dve.reciprocal(dis[:], dis[:]))
                dve.wait_ge(ld2, 9 * 16)
                link(dve.tensor_tensor(g_sb[:], g_sb[:], b_sb[:], ALU.add))
                dve.tensor_tensor(rz[:], g_sb[:, 0, 0:2, :], g_sb[:, 1, 0:2, :], ALU.add).then_inc(s_rdy, 1)
                dve.wait_ge(rz_rdy, 1)
                link(dve.tensor_tensor(nn[:], rz[:, 0, :], g_sb[:, 1, 2, :], ALU.mult))
                dve.tensor_tensor(nn[:], nn[:], g_sb[:, 0, 2, :], ALU.add).then_inc(n_rdy, 1)
                dve.wait_ge(t_rdy, 1)
                link(dve.tensor_tensor(tmp[:], h0[:], nn[:], ALU.subtract))
                link(dve.tensor_tensor(tmp[:], tmp[:], rz[:, 1, :], ALU.mult))
                link(dve.memset(weight[:], 0.0))
                link(dve.tensor_tensor(weight[0:C, :], tmp[:], nn[:], ALU.add))
                dve.wait_ge(rec_ld, 16)
                link(dve.tensor_copy(lo_e[:], rec_e[:, :, 0]))
                link(dve.tensor_copy(dst_e[:], rec_e[:, :, 1]))
                link(dve.tensor_copy(typ_e[:], rec_e[:, :, 2]))
                link(dve.memset(tab[:], 0.0))
                link(dve.tensor_copy(tab[:, :, 0:C], x0[:]))
                link(dve.memset(tab[:, :, ONE:ONE + 1], 1.0))

            @block.scalar
            def _(act):
                act.activation(dis[:], dis[:], ACT.Sqrt).then_inc(sq_rdy, 1)
                act.wait_ge(s_rdy, 1)
                act.activation(rz[:], rz[:], ACT.Sigmoid).then_inc(rz_rdy, 1)
                act.wait_ge(n_rdy, 1)
                act.activation(nn[:], nn[:], ACT.Tanh).then_inc(t_rdy, 1)

        def project(pe, dve, link, rhs, cols, take, s):
            in_rdy, tt_rdy, tt_cp, pr_rdy, pr_cp, ps_e, ps_a, seven, turned = s
            assert NB % 7 == 0

            def pe_part(b7):
                pe.wait_ge(in_rdy, b7 + 1)
                for j in range(7):
                    mm = pe.transpose(ps_e[:, j, :], seven[:, j, :], ident_f[:])
                mm.then_inc(tt_rdy, 1)
                pe.wait_ge(tt_cp, b7 + 1)
                for j in range(7):
                    mm = pe.matmul(ps_a[:, j, 0:cols], lhsT=turned[:, j, :], rhs=rhs[:, 0:cols], start=True, stop=True)
                mm.then_inc(pr_rdy, 1)

            if pe is not None:
                pe_part(0)
                with loop(pe, 1, NB // 7) as b7:
                    pe.wait_ge(pr_cp, b7)
                    pe_part(b7)
            else:
                def dve_part(b7):
                    dve.tensor_scalar(seven[:], tab[:, ds(b7 * 7, 7), :], 1.0, None, ALU.mult).then_inc(in_rdy, 1)
                    dve.wait_ge(tt_rdy, b7 + 1)
                    dve.tensor_copy(turned[:], ps_e[:, 0:7, :]).then_inc(tt_cp, 1)
                    dve.wait_ge(pr_rdy, b7 + 1)
                    take(b7).then_inc(pr_cp, 1)
                with loop(dve, 0, NB // 7) as b7:
                    dve_part(b7)

        for hop in range(2):
            with ExitStack() as ph:
                def sbh(name, shape, dt=F32):
                    return ph.enter_context(nc.sbuf_tensor(f"{name}_{hop}", shape, dt))

                def psh(name, shape, dt=F32):
                    return ph.enter_context(nc.psum_tensor(f"{name}_{hop}", shape, dt))

                def semh(name):
                    return ph.enter_context(nc.semaphore(f"{name}_{hop}"))

                acc = sbh("acc", [P, NB, C + 1])
                m_run = sbh("m_run", [P, NB])
                a_split = sbh("a_split", [P, NB, 3, R], BF16)
                st = ph.enter_context(ExitStack())
                a_all = st.enter_context(nc.sbuf_tensor(f"a_all_{hop}", [P, NB, 2 * R], F32))
                seven = st.enter_context(nc.sbuf_tensor(f"seven_{hop}", [P, 7, P], F32))
                turned = st.enter_context(nc.sbuf_tensor(f"turned_{hop}", [P, 7, P], F32))
                ps_e = st.enter_context(nc.psum_tensor(f"ps_e_{hop}", [P, 8, P], F32))
                ps_a = st.enter_context(nc.psum_tensor(f"ps_a_{hop}", [P, 8, P], F32))
                names = ("in_rdy", "tt_rdy", "tt_cp", "pr_rdy", "pr_cp")
                s = (*map(semh, names), ps_e, ps_a, seven, turned)
                tab_rdy, tab_st, dvt = semh("tab_rdy"), semh("tab_st"), semh("dvt")
                with nc.Block() as block:
                    @block.tensor
                    def _(pe):
                        project(pe, None, None, p12, 2 * R, None, s)

                    @block.vector
                    def _(dve):
                        link = Chain(dve, dvt)
                        dve.memset(acc[:], 0.0)
                        dve.memset(m_run[:], NO_SCORE)
                        project(None, dve, link, p12, 2 * R, lambda b7: dve.tensor_scalar(
                            a_all[:, ds(b7 * 7, 7), :], ps_a[:, 0:7, 0:2 * R], 1.0, None, ALU.mult), s)
                        dve.wait_ge(s[4], NB // 7)
                        dve.tensor_copy(tab[:, :, SC:SC + R], a_all[:, :, R:2 * R]).then_inc(tab_rdy, 1)
                        for j in range(3):
                            link(dve.tensor_copy(a_split[:, :, j, :], a_all[:, :, 0:R]))
                            if j < 2:
                                link(dve.tensor_tensor(a_all[:, :, 0:R], a_all[:, :, 0:R], a_split[:, :, j, :],
                                                       ALU.subtract))

                    @block.sync
                    def _(sp):
                        sp.wait_ge(tab_rdy, 1)
                        sp.dma_start(tab_d[hop].rearrange("(b p) w -> p b w", p=P), tab[:]).then_inc(tab_st, 16)
                        sp.wait_ge(tab_st, 16)
                st.close()

                stage_idx = sbh("stage_idx", [P, 2, 16], I32)
                rows = sbh("rows", [P, 8, KT, W])
                hot = sbh("hot", [P, 2, KT, P], BF16)
                hot_t = sbh("hot_t", [P, 2, GE], BF16)
                lower = sbh("lower", [P, 2, GE], BF16)
                picked = sbh("picked", [P, KT, R])
                s_raw = sbh("s_raw", [P, 2, KT])
                score = sbh("score", [P, 2, KT])
                masked = sbh("masked", [P, 2, GE])
                m_group = sbh("m_group", [P, 2])
                m_new = sbh("m_new", [P, 2])
                m_neg = sbh("m_neg", [P, 2])
                m_diff = sbh("m_diff", [P, 2, 2])
                alpha = sbh("alpha", [P, 2, 2])
                prob_t = sbh("prob_t", [P, 2, GE])
                prob = sbh("prob", [P, 2, GE])
                kept = sbh("kept", [P, 2, C + 1])
                inv = sbh("inv", [P, NB])
                sq = sbh("sq", [P, NB, C])
                ps_hot = psh("ps_hot", [P, 2 * GE], BF16)
                ps_x = psh("ps_x", [P, 2, 512])
                ps_s = psh("ps_s", [P, 2, GE])
                ps_p = psh("ps_p", [P, GE])
                ps_g = psh("ps_g", [P, 2, 512])
                (hot_rdy, hot_turned, hot_t_rdy, lower_rdy, x_rdy, score_rdy, s_spread, masked_rdy, exp_rdy, p_turned,
                 prob_rdy, summed, added, staged, tick, dvh, norm_sq, norm_rdy) = map(semh, (
                     "hot_rdy", "hot_turned", "hot_t_rdy", "lower_rdy", "x_rdy", "score_rdy", "s_spread", "masked_rdy",
                     "exp_rdy", "p_turned", "prob_rdy", "summed", "added", "staged", "tick", "dvh", "norm_sq",
                     "norm_rdy"))
                dtick = semh("dtick")
                landed = [semh(f"landed{i}") for i in range(8)]
                with nc.Block() as block:
                    @block.gpsimd
                    def _(pool):
                        def half(it, h):
                            g0 = it * 8 + h * 4
                            for g in range(4):
                                wait(pool, landed[h * 4 + g], it * 64)
                            wait_pool(pool, tick, summed, g0 - 7)
                            pool.tensor_copy(stage_idx[:, h, :], dst_e[:, ds(g0 * KT, 16)]).then_inc(staged, 1)
                            wait_pool(pool, tick, staged, it * 2 + h + 1)
                            for g in range(4):
                                if g:
                                    wait_pool(pool, tick, summed, g0 + g - 7)
                                for k in range(KT):
                                    j = g * KT + k
                                    pool.indirect_dma_start(
                                        out=rows[:, h * 4 + g, k, :], out_offset=None, in_=tab_d[hop],
                                        in_offset=bass.IndirectOffsetOnAxis(ap=stage_idx[:, h, j:j + 1], axis=0)
                                    ).then_inc(landed[h * 4 + g], 16)
                        for h in range(2):
                            half(0, h)
                        with loop(pool, 1, NG // 8) as it:
                            for h in range(2):
                                half(it, h)

                    @block.tensor
                    def _(pe):
                        def spread(g, p):
                            wait(pe, score_rdy, g + 1)
                            wait(pe, masked_rdy, g - 1)
                            for k in range(KT):
                                mm = pe.transpose(ps_s[:, p, k * P:(k + 1) * P],
                                                  score[:, p, k:k + 1].broadcast_to([P, P]), ident_f[:])
                            mm.then_inc(s_spread, 1)

                        def turn_prob(g, p):
                            wait(pe, exp_rdy, g + 1)
                            wait(pe, prob_rdy, g)
                            for k in range(KT):
                                mm = pe.transpose(ps_p[:, k * P:(k + 1) * P], prob_t[:, p, k * P:(k + 1) * P],
                                                  ident_f[:])
                            mm.then_inc(p_turned, 1)

                        def turn_hot(g, p):
                            wait(pe, hot_rdy, g + 1)
                            wait(pe, lower_rdy, g)
                            for k in range(KT):
                                mm = pe.transpose(ps_hot[:, k * P:(k + 1) * P], hot[:, p, k, :], ident_b[:])
                            mm.then_inc(hot_turned, 1)

                        def scores(g, p, u):
                            bb = pe.value_load(group_block[0:1, ds(g, 1)], min_val=0, max_val=NB - 1)
                            wait(pe, landed[u], (g - u) * 8 + 64)
                            wait(pe, hot_t_rdy, g + 1)
                            wait(pe, score_rdy, g - 1)
                            for k in range(KT):
                                for j in range(3):
                                    pe.matmul(ps_x[:, p, k * R:(k + 1) * R], lhsT=hot_t[:, p, k * P:(k + 1) * P],
                                              rhs=a_split[:, ds(bb, 1), j, :].rearrange("p a r -> p (a r)"),
                                              start=(k == 0 and j == 0), stop=False, skip_group_check=True)
                            mm = pe.matmul(ps_x[:, p, 0:KT * R], lhsT=ident_f[:], rhs=rows[:, u, :, SC:SC + R],
                                           start=False, stop=True, skip_group_check=True)
                            mm.then_inc(x_rdy, 1)

                        def sums(g, p, u):
                            wait(pe, prob_rdy, g + 1)
                            wait(pe, added, g - 1)
                            for k in range(KT):
                                mm = pe.matmul(ps_g[:, p, 0:C + 1], lhsT=prob[:, p, k * P:(k + 1) * P],
                                               rhs=rows[:, u, k, 0:C + 1], start=(k == 0), stop=(k == KT - 1))
                            mm.then_inc(summed, 1)

                        def body(i, u):
                            _, a, b, c = stages(i, NG)
                            if a:
                                turn_hot(i - 1, (u - 1) % 2)
                            if b:
                                spread(i - 2, u % 2)
                            if c:
                                turn_prob(i - 3, (u - 3) % 2)
                            if a:
                                scores(i - 1, (u - 1) % 2, (u - 1) % 8)
                            if c:
                                sums(i - 3, (u - 3) % 2, (u - 3) % 8)
                        pipelined(pe, NG, 3, 8, body)

                    @block.scalar
                    def _(act):
                        def body(i, u):
                            _, a, b, c = stages(i, NG)
                            p = (u - 1) % 2
                            if a:
                                g = i - 1
                                wait(act, hot_turned, g + 1)
                                wait(act, x_rdy, g - 1)
                                act.activation(hot_t[:, p, :], ps_hot[:, 0:GE], ACT.Copy).then_inc(hot_t_rdy, 1)
                                wait(act, masked_rdy, g - 1)
                                act.activation(lower[:, p, :], ps_hot[:, 0:GE], ACT.Copy, bias=-BIG, scale=BIG
                                               ).then_inc(lower_rdy, 1)
                            if c:
                                g = i - 3
                                wait(act, p_turned, g + 1)
                                wait(act, summed, g - 1)
                                act.activation(prob[:, p, :], ps_p[:], ACT.Copy).then_inc(prob_rdy, 1)
                            if b:
                                g, q = i - 2, 1 - p
                                wait(act, masked_rdy, g + 1)
                                wait(act, p_turned, g - 1)
                                act.activation(prob_t[:, q, :], masked[:, q, :], ACT.Exp, bias=m_neg[:, q:q + 1])
                                wait(act, added, g - 1)
                                act.activation(alpha[:, q, :], m_diff[:, q, :], ACT.Exp).then_inc(exp_rdy, 1)
                        pipelined(act, NG, 3, 8, body)
                        act.wait_ge(norm_sq, 1)
                        act.activation(inv[:], inv[:], ACT.Sqrt).then_inc(norm_rdy, 1)

                    @block.vector
                    def _(dve):
                        link = Chain(dve, dvh)

                        def one_hot(i, u):
                            wait(dve, hot_turned, i - 1)
                            for k in range(KT):
                                ins = dve.tensor_scalar(hot[:, u % 2, k, :], iota_b[:, 0:P],
                                                        lo_e[:, ds(i * KT + k, 1)], None, ALU.is_equal)
                            ins.then_inc(hot_rdy, 1)

                        def mask(g, p):
                            bb = dve.value_load(group_block[0:1, ds(g, 1)], min_val=0, max_val=NB - 1)
                            wait(dve, lower_rdy, g + 1)
                            wait(dve, exp_rdy, g - 1)
                            wait(dve, s_spread, g + 1)
                            dve.sem_inc(dtick, 1)
                            link(dve.tensor_tensor_reduce(masked[:, p, :], lower[:, p, :], ps_s[:, p, :], 1.0, -3e38,
                                                          ALU.add, ALU.max, m_group[:, p:p + 1]))
                            link(dve.tensor_tensor(m_new[:, p:p + 1], m_run[:, ds(bb, 1)], m_group[:, p:p + 1], ALU.max))
                            dve.tensor_tensor(m_diff[:, p, 0:1], m_run[:, ds(bb, 1)], m_new[:, p:p + 1], ALU.subtract)
                            dve.tensor_tensor(m_diff[:, p, 1:2], m_group[:, p:p + 1], m_new[:, p:p + 1], ALU.subtract)
                            link(dve.tensor_scalar(m_neg[:, p:p + 1], m_group[:, p:p + 1], -1.0, None, ALU.mult))
                            link(dve.tensor_scalar(m_run[:, ds(bb, 1)], m_new[:, p:p + 1], 1.0, None, ALU.mult))
                            dve.sem_inc(masked_rdy, 1)

                        def combine(g, p):
                            bb = dve.value_load(group_block[0:1, ds(g, 1)], min_val=0, max_val=NB - 1)
                            a = acc[:, ds(bb, 1), :].rearrange("p a c -> p (a c)")
                            wait(dve, summed, g + 1)
                            wait(dve, exp_rdy, g + 1)
                            link(dve.tensor_scalar(kept[:, p, :], a, alpha[:, p, 0:1], None, ALU.mult))
                            link(dve.scalar_tensor_tensor(out=a, in0=ps_g[:, p, 0:C + 1], scalar=alpha[:, p, 1:2],
                                                          in1=kept[:, p, :], op0=ALU.mult, op1=ALU.add))
                            dve.sem_inc(added, 1)

                        def select(g, p):
                            wait(dve, x_rdy, g + 1)
                            for k in range(KT):
                                link.mark(dve.scalar_tensor_tensor(
                                    out=picked[:, k, :], in0=iota_f[:, 0:R], scalar=typ_e[:, ds(g * KT + k, 1)],
                                    in1=ps_x[:, p, k * R:(k + 1) * R], op0=ALU.is_equal, op1=ALU.mult,
                                    accum_out=s_raw[:, p, k:k + 1]))
                            link.sync()
                            wait(dve, s_spread, g - 1)
                            dve.scalar_tensor_tensor(out=score[:, p, :], in0=s_raw[:, p, :], scalar=0.2,
                                                     in1=s_raw[:, p, :], op0=ALU.mult, op1=ALU.max
                                                     ).then_inc(score_rdy, 1)

                        def body(i, u):
                            z, a, b, c = stages(i, NG)
                            if b:
                                mask(i - 2, u % 2)
                            if z:
                                one_hot(i, u)
                            if a:
                                select(i - 1, (u - 1) % 2)
                            if c:
                                combine(i - 3, (u - 3) % 2)
                        pipelined_counted(dve, link, NG, 3, 8, body)
                        emb = tab[:, :, 0:C]
                        dve.wait_ge(added, NG)
                        link(dve.tensor_scalar(inv[:], acc[:, :, C], 0.5, None, ALU.max))
                        link(dve.reciprocal(inv[:], inv[:]))
                        link(dve.tensor_tensor(sq[:], acc[:, :, 0:C], inv[:].unsqueeze(2).broadcast_to([P, NB, C]), ALU.mult))
                        link(dve.tensor_tensor(emb, emb, sq[:], ALU.add))
                        link(dve.tensor_tensor(sq[:], emb, emb, ALU.mult))
                        link(dve.tensor_reduce(inv[:], sq[:], AX, ALU.add))
                        dve.tensor_scalar(inv[:], inv[:], 1e-24, None, ALU.max).then_inc(norm_sq, 1)
                        dve.wait_ge(norm_rdy, 1)
                        link(dve.reciprocal(inv[:], inv[:]))
                        link(dve.tensor_tensor(emb, emb, inv[:].unsqueeze(2).broadcast_to([P, NB, C]), ALU.mult))

        with ExitStack() as ph:
            def sbl(name, shape, dt=F32):
                return ph.enter_context(nc.sbuf_tensor(name, shape, dt))

            def psl(name, shape, dt=F32):
                return ph.enter_context(nc.psum_tensor(name, shape, dt))

            def seml(name):
                return ph.enter_context(nc.semaphore(name))

            y = sbl("y", [P, NB, C])
            total = sbl("total", [P, AB, C])
            cen = sbl("cen", [P, NB, C])
            ssq = sbl("ssq", [P, NB, C])
            mean = sbl("mean", [P, NB])
            var = sbl("var", [P, NB])
            eps = sbl("eps", [P, 1])
            seven = sbl("seven", [P, 7, P])
            turned = sbl("turned", [P, 7, P])
            rows = sbl("y_rows", [P, 4, KT, C])
            stage_idx = sbl("stage_src", [P, 2, 16], I32)
            near = sbl("near", [P, 2, KT, 2 * P])
            var_rdy, sd_rdy = seml("var_rdy"), seml("sd_rdy")

            def layernorm(dve, link, n):
                link(dve.tensor_reduce(mean[:], x0[:], AX, ALU.add))
                link(dve.tensor_scalar(mean[:], mean[:], 1.0 / C, None, ALU.mult))
                link(dve.tensor_tensor(cen[:], x0[:], mean[:].unsqueeze(2).broadcast_to([P, NB, C]), ALU.subtract))
                link(dve.tensor_tensor(ssq[:], cen[:], cen[:], ALU.mult))
                link(dve.tensor_reduce(var[:], ssq[:], AX, ALU.add))
                dve.tensor_scalar(var[:], var[:], 1.0 / C, 1e-5, ALU.mult, ALU.add).then_inc(var_rdy, 1)
                dve.wait_ge(sd_rdy, n)
                link(dve.reciprocal(var[:], var[:]))
                link(dve.tensor_tensor(x0[:], cen[:], var[:].unsqueeze(2).broadcast_to([P, NB, C]), ALU.mult))

            def root(act, n):
                act.wait_ge(var_rdy, n)
                act.activation(var[:], var[:], ACT.Sqrt).then_inc(sd_rdy, 1)

            with ExitStack() as st:
                ps_e = st.enter_context(nc.psum_tensor("ps_e_y", [P, 8, P], F32))
                ps_a = st.enter_context(nc.psum_tensor("ps_a_y", [P, 8, P], F32))
                s = (*map(seml, ("in_rdy_y", "tt_rdy_y", "tt_cp_y", "pr_rdy_y", "pr_cp_y")), ps_e, ps_a, seven, turned)
                x_set, y_rdy, y_st, dvy = map(seml, ("x_set", "y_rdy", "y_st", "dvy"))
                with nc.Block() as block:
                    @block.vector
                    def _(dve):
                        link = Chain(dve, dvy)
                        dve.memset(total[:], 0.0)
                        link(dve.tensor_tensor(x0[:], x0[:], tab[:, :, 0:C], ALU.add))
                        layernorm(dve, link, 1)
                        dve.tensor_copy(tab[:, :, 0:C], x0[:]).then_inc(x_set, 1)
                        dve.wait_ge(x_set, 1)
                        project(None, dve, link, weight, C, lambda b7: dve.tensor_scalar(
                            y[:, ds(b7 * 7, 7), :], ps_a[:, 0:7, 0:C], 1.0, None, ALU.mult), s)
                        dve.wait_ge(s[4], NB // 7)
                        link(dve.tensor_tensor(y[:], y[:], dis[:].unsqueeze(2).broadcast_to([P, NB, C]), ALU.mult))
                        dve.sem_inc(y_rdy, 1)

                    @block.scalar
                    def _(act):
                        root(act, 1)

                    @block.tensor
                    def _(pe):
                        pe.wait_ge(x_set, 1)
                        project(pe, None, None, weight, C, None, s)

                    @block.sync
                    def _(sp):
                        sp.wait_ge(y_rdy, 1)
                        sp.dma_start(y_d.rearrange("(b p) w -> p b w", p=P), y[:]).then_inc(y_st, 16)
                        sp.wait_ge(y_st, 16)

            ps_g = psl("ps_gy", [P, 2, 512])
            near_rdy, summed, added, staged, tick, dvl, fin_rdy, out_st = map(seml, (
                "near_rdy", "summed_y", "added_y", "staged_y", "tick_y", "dvl", "fin_rdy", "out_st"))
            landed = [seml(f"landed_y{i}") for i in range(4)]
            dtick_l = seml("dtick_l")
            AHEAD = 4
            with nc.Block() as block:
                @block.gpsimd
                def _(pool):
                    sweeps = pool.value_load(n_sweeps[0:1, 0:1], min_val=1, max_val=NB // 2 + 1)
                    with loop(pool, 0, sweeps) as w:
                        with loop(pool, 0, NGD // 8) as it:
                            for h in range(2):
                                f0 = w * NGD + it * 8 + h * 4
                                wait_pool(pool, tick, summed, f0 - 3 + AHEAD)
                                pool.tensor_copy(stage_idx[:, h, :], src_cols[:, ds(it * 8 + h * 4, 4), :]
                                                 .rearrange("p g k -> p (g k)")).then_inc(staged, 1)
                                wait_pool(pool, tick, staged, w * (NGD // 4) + it * 2 + h + 1)
                                for g in range(4):
                                    if g:
                                        wait_pool(pool, tick, summed, f0 + g - 3 + AHEAD)
                                    for k in range(KT):
                                        j = g * KT + k
                                        pool.indirect_dma_start(
                                            out=rows[:, g, k, :], out_offset=None, in_=y_d,
                                            in_offset=bass.IndirectOffsetOnAxis(ap=stage_idx[:, h, j:j + 1], axis=0)
                                        ).then_inc(landed[g], 16)

                @block.tensor
                def _(pe):
                    pe.sem_inc(summed, AHEAD)
                    sweeps = pe.value_load(n_sweeps[0:1, 0:1], min_val=1, max_val=NB // 2 + 1)
                    with loop(pe, 0, sweeps) as w:
                        with loop(pe, 0, NGD - 3, 4) as i0:
                            for u in range(4):
                                f = w * NGD + i0 + u
                                pe.wait_ge(landed[u], (w * NGD + i0) * 16 + 64)
                                pe.wait_ge(near_rdy, f + 1)
                                pe.wait_ge(added, f - 1 + AHEAD)
                                for j in range(2):
                                    for k in range(KT):
                                        mm = pe.matmul(ps_g[:, u % 2, j * C:(j + 1) * C], lhsT=near[:, u % 2, k, j * P:(j + 1) * P],
                                                       rhs=rows[:, u, k, :], start=(k == 0), stop=(k == KT - 1))
                                mm.then_inc(summed, 1)

                @block.vector
                def _(dve):
                    link = Chain(dve, dvl)
                    dve.sem_inc(added, AHEAD)
                    sweeps = dve.value_load(n_sweeps[0:1, 0:1], min_val=1, max_val=NB // 2 + 1)

                    def windows(i, f, u):
                        dve.wait_ge(summed, f - 1 + AHEAD)
                        for k in range(KT):
                            ins = dve.tensor_scalar(near[:, u % 2, k, :], iota_f[:, 0:2 * P], rel_dst[:, ds(i, 1), k],
                                                    None, ALU.is_equal)
                        ins.then_inc(near_rdy, 1)

                    def add(i, f, w, u):
                        first = dve.value_load(window0[0:1, ds(i, 1)], min_val=0, max_val=NB - 1)
                        t = total[:, ds(first + w * 2, 2), :]
                        dve.wait_ge(summed, f + 1 + AHEAD)
                        dve.wait_ge(added, f + AHEAD)
                        dve.tensor_tensor(t, t, ps_g[:, u % 2, 0:2 * C].rearrange("p (j c) -> p j c", j=2), ALU.add).then_inc(added, 1)

                    with loop(dve, 0, sweeps) as w:
                        f0 = w * NGD
                        windows(0, f0, 0)
                        for u in range(1, 4):
                            windows(u, f0 + u, u)
                            add(u - 1, f0 + u - 1, w, u - 1)
                        with loop(dve, 4, NGD - 3, 4) as i0:
                            for u in range(4):
                                windows(i0 + u, f0 + i0 + u, u)
                                add(i0 + u - 1, f0 + i0 + (u - 1), w, u - 1)
                        add(NGD - 1, f0 + NGD - 1, w, 3)
                        dve.tensor_scalar(rel_dst[:], rel_dst[:], -2.0 * P, None, ALU.add).then_inc(dvl, 1)
                        dve.wait_ge(dvl, w + 1)
                        dve.sem_inc(dtick_l, 1)

                    link.base = sweeps
                    link(dve.tensor_tensor(y[:], y[:], total[:, 0:NB, :], ALU.add))
                    link(dve.tensor_tensor(y[:], y[:], dis[:].unsqueeze(2).broadcast_to([P, NB, C]), ALU.mult))
                    link(dve.tensor_scalar(y[:], y[:], 0.0, None, ALU.max))
                    link(dve.tensor_tensor(x0[:], x0[:], y[:], ALU.add))
                    layernorm(dve, link, 2)
                    dve.sem_inc(fin_rdy, 1)

                @block.scalar
                def _(act):
                    root(act, 2)

                @block.sync
                def _(sp):
                    sp.wait_ge(fin_rdy, 1)
                    sp.dma_start(out[0:FULL * P].rearrange("(b p) c -> p b c", p=P), x0[:, 0:FULL, :]).then_inc(out_st, 16)
                    sp.dma_start(out[FULL * P:N], x0[0:REST, FULL, :]).then_inc(out_st, 16)
                    sp.wait_ge(out_st, 32)


def kernel(**inputs):
    import numpy as np
    import concourse.bacc as bacc
    from concourse.bass_utils import run_bass_kernel_spmd

    def turned(w):
        r, k = w.shape
        return np.ascontiguousarray(w.reshape(r // 512, 512, k // 512, 4, 128).transpose(0, 2, 4, 3, 1))

    a = {k: np.asarray(v) for k, v in inputs.items()}
    arrays = {
        "x": a["x"], "src": a["src"], "dst": a["dst"], "typ": a["edge_type_50"],
        "relT": np.ascontiguousarray(a["L0_gnn_relation_emb"].T),
        "fc_w": a["L0_gnn_fc_w"], "fc_b": np.ascontiguousarray(a["L0_gnn_fc_b"][:, None]),
        "w_ih": turned(a["L1_gnn_w_ih"]), "w_hh": turned(a["L1_gnn_w_hh"]),
        "h_col": np.ascontiguousarray(a["L1_gnn_initial_weight"].reshape(-1, 128).T),
        "h_mat": a["L1_gnn_initial_weight"],
        "b_ih": a["L1_gnn_b_ih"], "b_hh": a["L1_gnn_b_hh"],
    }
    nc = bacc.Bacc("TRN2", target_bir_lowering=False, num_devices=1)
    args = [nc.dram_tensor(k, v.shape, mybir.dt.from_np(v.dtype), kind="ExternalInput").ap() for k, v in arrays.items()]
    out = nc.dram_tensor("out", a["x"].shape, F32, kind="ExternalOutput").ap()
    gnn_kernel(nc, *args, out)
    r = run_bass_kernel_spmd(nc, [arrays], core_ids=[0])
    return r.results[0]["out"]
```

```python
from contextlib import ExitStack

import concourse.bass as bass
from concourse import mybir

ALU = mybir.AluOpType
ACT = mybir.ActivationFunctionType
AX = mybir.AxisListType.X
F32 = mybir.dt.float32
BF16 = mybir.dt.bfloat16
I32 = mybir.dt.int32

P = 128
BIG = float(2.0 ** 100)
NO_SCORE = -float(2.0 ** 97)
PAD_DST = 30000
PAD_LO = 200
KT = 4
GE = KT * P


def ds(start, n):
    return bass.ds(start, n)


def loop(eng, lo, hi, step=1):
    return eng.bass.Fori(lo, hi, step, engines=(eng.engine,), hint_back_edge=True)


def wait(eng, sem, value):
    if isinstance(value, int) and value <= 0:
        return
    eng.wait_ge(sem, value)


def wait_pool(pool, tick, sem, value):
    if isinstance(value, int) and value <= 0:
        return
    pool.wait_ge(sem, value)
    pool.sem_inc(tick, 1)


class Chain:

    def __init__(self, eng, sem, tick=None):
        self.eng, self.sem, self.tick, self.base, self.n = eng, sem, tick, 0, 0

    def __call__(self, ins):
        self.n += 1
        ins.then_inc(self.sem, 1)
        self.eng.wait_ge(self.sem, self.base + self.n)

    def mark(self, ins):
        self.n += 1
        ins.then_inc(self.sem, 1)

    def sync(self):
        self.eng.wait_ge(self.sem, self.base + self.n)

    def loop(self, lo, hi, per, body):
        before = self.base + self.n
        with loop(self.eng, lo, hi) as i:
            self.base, self.n = (i - lo) * per + before if lo else i * per + before, 0
            body(i)
            self.eng.sem_inc(self.tick, 1)
            assert self.n == per, (self.n, per)
        self.base, self.n = before + (hi - lo) * per, 0


BLOCK_BACK = 4


def blocks_from(eng, table, i0, n, top):
    _, v = eng.bass.values_load_multi_w_load_instructions(
        table[0:1, ds(i0 + BLOCK_LEAD - BLOCK_BACK, n + BLOCK_BACK)], engines=(eng.engine,), min_val=0, max_val=top,
        skip_runtime_bounds_check_because="the table is held below the number of blocks")
    return v


BLOCK_LEAD = 8
LAG = 3
UNROLL = 8


def pipelined(eng, n, body, table=None, top=0, link=None):
    def steps(i0, count, flags):
        v = blocks_from(eng, table, i0, UNROLL if count == UNROLL else 0, top) if table is not None else None
        for u in range(count):
            body(i0 + u, u, flags(u), (lambda d, u=u: v[BLOCK_BACK + u - d]))

    steps(0, UNROLL, lambda u: (True, u >= 1, u >= 2, u >= 3))
    before = link.base + link.n if link else 0
    with loop(eng, UNROLL, n - UNROLL + 1, UNROLL) as i0:
        if link:
            link.base, link.n = (i0 - UNROLL) * PER_GROUP + before, 0
        steps(i0, UNROLL, lambda u: (True,) * 4)
        assert not link or link.n == PER_GROUP * UNROLL, link.n
    if link:
        link.base, link.n = (n - UNROLL) * PER_GROUP + before, 0
    steps(n, LAG, lambda u: (False, u < 1, u < 2, True))


PER_GROUP = 8


def gnn_kernel(nc, x, src, dst, typ, relT, fc_w, fc_b, w_ih, w_hh, h_col, h_mat, b_ih, b_hh, out):
    N, C = x.shape
    E = src.shape[0]
    R = relT.shape[1]
    NB = -(-N // P)
    FULL, REST = N // P, N % P
    PS = 125
    ES = E // PS
    CH = 5
    EC = ES // CH
    assert PS * ES == E and EC * CH == ES and EC % 32 == 0
    NG0 = -(-(E + NB * (GE - 1)) // GE)
    NG = -(-NG0 // 8) * 8
    T1 = NG * KT
    MIN_ROUNDS = -(-(-(-E // GE)) // UNROLL)
    NGD = -(-(-(-E // GE)) // 8) * 8
    GP = NGD // 4
    GLAST = E // GE
    TD = NGD * KT
    W = 128
    ONE, SC = C, C + 1
    FLAT = C * C
    KC = FLAT // P
    RC = 3 * FLAT // 512
    PC = KC // 4
    RING = 4
    AB = 2 * NB + 2

    with ExitStack() as ctx:
        def sb(name, shape, dt=F32):
            return ctx.enter_context(nc.sbuf_tensor(name, shape, dt))

        def sem(name):
            return ctx.enter_context(nc.semaphore(name))

        rec_d = nc.dram_tensor("rec_d", (P * T1, 4), I32).ap()
        tab_d = [nc.dram_tensor(f"tab{h}_d", (NB * P, W), F32).ap() for h in range(2)]
        y_d = nc.dram_tensor("y_d", (NB * P, C), F32).ap()
        gate_d = nc.dram_tensor("gate_d", (2 * RC, 512), F32).ap()

        iota_f = sb("iota_f", [P, 512])
        iota_b = sb("iota_b", [P, 256], BF16)
        ident_f = sb("ident_f", [P, P])
        ident_b = sb("ident_b", [P, P], BF16)
        x0 = sb("x0", [P, NB, C])
        p12 = sb("p12", [P, 2 * R])
        group_block = sb("group_block", [P, BLOCK_LEAD + NG], I32)
        n_extra = sb("n_extra", [P, 1], I32)
        window0 = sb("window0", [P, NGD], I32)
        n_sweeps = sb("n_sweeps", [P, 1], I32)
        rel_dst = sb("rel_dst", [P, NGD, KT])
        src_cols = sb("src_cols", [P, NGD, KT], I32)
        dis = sb("dis", [P, NB])
        weight = sb("weight", [P, C])
        const_rdy = sem("const_rdy")

        with ExitStack() as ph:
            def sb1(name, shape, dt=F32):
                return ph.enter_context(nc.sbuf_tensor(name, shape, dt))

            def ps1(name, shape, dt=F32):
                return ph.enter_context(nc.psum_tensor(name, shape, dt))

            def sem1(name):
                return ph.enter_context(nc.semaphore(name))

            iota_i = sb1("iota_i", [P, 512], I32)
            part_i = sb1("part_i", [P, 1], I32)
            part_f = sb1("part_f", [P, 1])
            tri = sb1("tri", [P, P])
            ones = sb1("ones", [P, P])
            idx_i = sb1("idx_i", [PS, 3, ES], I32)
            blk_b = sb1("blk_b", [PS, ES], BF16)
            rec = sb1("rec", [PS, ES, 4], I32)
            one_b = sb1("one_b", [PS, ES], BF16)
            mask_b = sb1("mask_b", [PS, ES], BF16)
            buf_a = sb1("buf_a", [P, max(ES, TD)])
            buf_b = sb1("buf_b", [P, max(ES, TD)])
            cum, pos = buf_a[0:PS, 0:ES], buf_b[0:PS, 0:ES]
            row = sb1("row", [PS, ES], I32)
            counts = sb1("counts", [PS, NB])
            base = sb1("base", [PS, NB])
            tot = sb1("tot", [P, NB])
            n_groups_i = sb1("n_groups_i", [P, NB], I32)
            n_groups = sb1("n_groups", [P, NB])
            end_group = sb1("end_group", [P, NB])
            gb = sb1("gb", [P, NG])
            blank = sb1("blank", [P, 32, 4], I32)
            stage_row = sb1("stage_row", [PS, 2, 16], I32)
            stage_rec = sb1("stage_rec", [PS, 2, 16, 4], I32)
            grp_dst = sb1("grp_dst", [GP, 4, GE], I32)
            grp_src = sb1("grp_src", [GP, 4, GE], I32)
            grp_f = sb1("grp_f", [GP, 4, GE])
            grp_hi = sb1("grp_hi", [GP, 4, GE])
            lowest = sb1("lowest", [GP, 4])
            highest = sb1("highest", [GP, 4])
            span = sb1("span", [GP, 1])
            dst_t = sb1("dst_t", [P, NGD, KT])
            dst_ti = sb1("dst_ti", [P, NGD, KT], I32)
            lo_t, hi_t = buf_a[:, 0:TD], buf_b[:, 0:TD]
            win_f = sb1("win_f", [P, NGD])
            sw_f = sb1("sw_f", [P, 1])
            deg = sb1("deg", [P, NB])
            lo_hot = sb1("lo_hot", [P, 8, P], BF16)
            hi_hot = sb1("hi_hot", [P, 8, 64], BF16)
            h_sb = sb1("h_sb", [P, KC])
            ring = sb1("ring", [P, RING, 4, 512])
            gate_row = sb1("gate_row", [1, 2, 512])

            ps_small = ps1("ps_small", [P, 2, 256])
            ps_t = ps1("ps_t", [P, 2, 512])
            ps_gate = ps1("ps_gate", [1, 2, 512])
            ps_deg = ps1("ps_deg", [P, 512])

            iota_rdy, idx_ld, grp_ld, h_ld, x_ld = map(sem1, ("iota_rdy", "idx_ld", "grp_ld", "h_ld", "x_ld"))
            dv, blank_rdy, blank_st, grp_set = map(sem1, ("dv", "blank_rdy", "blank_st", "grp_set"))
            cnt_rdy, pre_rdy, row_rdy, rec_rdy = map(sem1, ("cnt_rdy", "pre_rdy", "row_rdy", "rec_rdy"))
            grp_rdy, tp_rdy, tp_used, lim_rdy, lim_t = map(sem1, ("grp_rdy", "tp_rdy", "tp_used", "lim_rdy", "lim_t"))
            staged, tick = sem1("staged"), sem1("tick")
            scattered = [sem1(f"scattered{h}") for h in range(2)]
            piece_ld = [sem1(f"piece_ld{i}") for i in range(RING)]
            piece_used, gate_cp = sem1("piece_used"), sem1("gate_cp")
            gate_st = [sem1(f"gate_st{i}") for i in range(2)]
            dtick1 = sem1("dtick1")
            hot_rdy, hot_used = sem1("hot_rdy"), sem1("hot_used")

            block = ph.enter_context(nc.Block())

            @block.sync
            def _(sp):
                for i, v in enumerate((src, dst, typ)):
                    sp.dma_start(idx_i[:, i, :], v.rearrange("(p t) -> p t", p=PS)).then_inc(idx_ld, 16)
                sp.wait_ge(grp_set, 2)
                for v, t in ((dst, grp_dst), (src, grp_src)):
                    for c in range(4):
                        n = min(GP, GLAST - c * GP)
                        sp.dma_start(t[0:n, c, :], v[c * GP * GE:(c * GP + n) * GE].rearrange("(p e) -> p e", e=GE)
                                     ).then_inc(grp_ld, 16)
                    n = E - GLAST * GE
                    sp.dma_start(t[GLAST - 3 * GP:GLAST - 3 * GP + 1, 3, 0:n],
                                 v[GLAST * GE:E].rearrange("(p e) -> p e", p=1)).then_inc(grp_ld, 16)
                sp.dma_start(h_sb[:], h_col).then_inc(h_ld, 16)
                for m, w in enumerate((w_ih, w_hh)):
                    def pieces(n):
                        for pc in range(PC):
                            wait(sp, piece_used, (m * RC + n) * PC + pc - RING + 1)
                            sp.dma_start(ring[:, pc % RING].rearrange("p q c -> p (q c)"),
                                         w[ds(n, 1), pc].rearrange("a p q c -> (a p) (q c)")).then_inc(piece_ld[pc % RING], 16)
                    if m == 0:
                        pieces(0)
                    with loop(sp, 1 - m, RC) as n:
                        pieces(n)

            @block.gpsimd
            def _(pool):
                pool.iota(iota_i[:], pattern=[[1, 512]], base=0, channel_multiplier=0).then_inc(iota_rdy, 1)
                pool.iota(part_i[:], pattern=[[0, 1]], base=0, channel_multiplier=1).then_inc(iota_rdy, 1)
                pool.memset(grp_dst[:], PAD_DST).then_inc(grp_set, 1)
                pool.memset(grp_src[:], 0).then_inc(grp_set, 1)

                def batch(b, h, first):
                    if not first:
                        wait_pool(pool, tick, scattered[h], b * 256)
                    t0 = b * 32 + h * 16
                    pool.tensor_copy(stage_row[:, h, :], row[:, ds(t0, 16)]).then_inc(staged, 1)
                    pool.tensor_copy(stage_rec[:, h], rec[:, ds(t0, 16), :]).then_inc(staged, 1)
                    wait_pool(pool, tick, staged, b * 4 + h * 2 + 2)
                    for j in range(16):
                        pool.indirect_dma_start(
                            out=rec_d, out_offset=bass.IndirectOffsetOnAxis(ap=stage_row[:, h, j:j + 1], axis=0),
                            in_=stage_rec[:, h, j, :], in_offset=None).then_inc(scattered[h], 16)

                pool.wait_ge(row_rdy, 1)
                pool.wait_ge(rec_rdy, 3)
                pool.wait_ge(blank_st, 16)
                for h in range(2):
                    batch(0, h, True)
                for c in range(CH):
                    if c:
                        pool.wait_ge(row_rdy, c + 1)
                    with loop(pool, max(1, c * EC // 32), (c + 1) * EC // 32) as b:
                        for h in range(2):
                            batch(b, h, False)
                for h in range(2):
                    pool.wait_ge(scattered[h], ES // 32 * 256)

            @block.scalar
            def _(act):
                act.wait_ge(blank_rdy, 2)
                act.dma_start(rec_d.rearrange("(p t) f -> p t f", p=P).rearrange("p (a b) f -> p a (b f)", b=32),
                              blank[:].rearrange("p b f -> p (b f)").unsqueeze(1).broadcast_to([P, T1 // 32, 128])
                              ).then_inc(blank_st, 16)
                act.wait_ge(x_ld, 1)
                act.dma_start(x0[:, 0:FULL, :], x[0:FULL * P].rearrange("(b p) c -> p b c", p=P)).then_inc(x_ld, 16)
                act.dma_start(x0[0:REST, FULL, :], x[FULL * P:N]).then_inc(x_ld, 16)
                act.wait_ge(idx_ld, 48)
                act.activation(rec[:, :, 1], idx_i[:, 1, :], ACT.Copy).then_inc(rec_rdy, 1)
                act.activation(rec[:, :, 2], idx_i[:, 2, :], ACT.Copy).then_inc(rec_rdy, 1)

                def evacuate(k, s):
                    act.wait_ge(piece_used, (k + 1) * PC)
                    act.activation(gate_row[:, s, :], ps_gate[:, s, :], ACT.Copy).then_inc(gate_cp, 1)
                    act.wait_ge(gate_cp, k + 1)
                    act.dma_start(gate_d[ds(k, 1), :], gate_row[:, s, :]).then_inc(gate_st[s], 16)

                for s in range(2):
                    evacuate(s, s)
                with loop(act, 1, RC) as k2:
                    for s in range(2):
                        act.wait_ge(gate_st[s], k2 * 16)
                        evacuate(k2 * 2 + s, s)
                for s in range(2):
                    act.wait_ge(gate_st[s], RC * 16)
                act.wait_ge(x_ld, 33)

            @block.tensor
            def _(pe):
                pe.wait_ge(const_rdy, 1)
                pe.wait_ge(cnt_rdy, 1)
                pe.matmul(ps_small[0:PS, 0, 0:NB], lhsT=tri[0:PS, 0:PS], rhs=counts[:], start=True, stop=True)
                pe.matmul(ps_small[:, 1, 0:NB], lhsT=ones[0:PS, :], rhs=counts[:], start=True, stop=True
                          ).then_inc(pre_rdy, 1)
                for i in range(2 * 4 * KT):
                    v, c, k = i // (4 * KT), i // KT % 4, i % KT
                    pe.wait_ge(grp_rdy, v + 1)
                    wait(pe, tp_used, i - 1)
                    pe.transpose(ps_t[:, i % 2, 0:GP], grp_f[:, c, k * P:(k + 1) * P] if v == 0 else
                                 grp_hi[:, c, k * P:(k + 1) * P], ident_f[0:GP, 0:GP]).then_inc(tp_rdy, 1)
                pe.wait_ge(h_ld, 16)

                def chunk(k, s):
                    for pc in range(PC):
                        pe.wait_ge(piece_ld[pc % RING], k * (PC // RING * 16) + (pc // RING + 1) * 16)
                        if pc == 0:
                            wait(pe, gate_cp, k - 1)
                        for q in range(4):
                            kc = pc * 4 + q
                            mm = pe.matmul(ps_gate[:, s, :], lhsT=h_sb[:, kc:kc + 1], rhs=ring[:, pc % RING, q, :],
                                           start=(kc == 0), stop=(kc == KC - 1))
                        mm.then_inc(piece_used, 1)

                for s in range(2):
                    chunk(s, s)
                with loop(pe, 2, 2 * RC - 1, 2) as k0:
                    for s in range(2):
                        chunk(k0 + s, s)
                pe.wait_ge(lim_rdy, 1)
                for c in range(4):
                    pe.transpose(ps_t[:, 0, c * GP:(c + 1) * GP], lowest[:, c:c + 1].broadcast_to([GP, P]),
                                 ident_f[0:GP, 0:GP])
                pe.transpose(ps_t[:, 1, 0:GP], span[:].broadcast_to([GP, P]), ident_f[0:GP, 0:GP]).then_inc(lim_t, 1)
                def count(i, j, first=False, last=False):
                    pe.matmul(ps_deg[:, 0:NB], lhsT=lo_hot[:, j, :], rhs=hi_hot[:, j, 0:NB], start=first,
                              stop=last, skip_group_check=True).then_inc(hot_used, 1)
                pe.wait_ge(hot_rdy, 1)
                for j in range(8):
                    pe.wait_ge(hot_rdy, j + 1)
                    count(0, j, first=(j == 0))
                with loop(pe, 8, TD - 15, 8) as t0:
                    for j in range(8):
                        pe.wait_ge(hot_rdy, t0 + j + 1)
                        count(t0, j)
                for j in range(8):
                    pe.wait_ge(hot_rdy, TD - 8 + j + 1)
                    count(0, j, last=(j == 7))

            @block.vector
            def _(dve):
                link = Chain(dve, dv, dtick1)
                dve.memset(ones[:], 1.0)
                dve.memset(one_b[:], 1.0)
                dve.memset(pos, 0.0)
                dve.memset(gb[:], 0.0)
                link.mark(dve.memset(blank[:], 0))
                link.sync()
                dve.memset(blank[:, :, 0], PAD_LO).then_inc(blank_rdy, 2)
                dve.memset(x0[:], 0.0).then_inc(x_ld, 1)
                link(dve.memset(rec[:, :, 3], 0))
                dve.wait_ge(iota_rdy, 2)
                dve.tensor_copy(iota_b[:], iota_i[:, 0:256])
                dve.tensor_copy(iota_f[:], iota_i[:])
                link(dve.tensor_copy(part_f[:], part_i[:]))
                link.mark(dve.tensor_scalar(ident_f[:], iota_f[:, 0:P], part_f[:], None, ALU.is_equal))
                link.mark(dve.tensor_scalar(ident_b[:], iota_f[:, 0:P], part_f[:], None, ALU.is_equal))
                link(dve.tensor_scalar(tri[:], iota_f[:, 0:P], part_f[:], None, ALU.is_gt))
                dve.sem_inc(const_rdy, 1)
                dve.wait_ge(idx_ld, 48)
                link(dve.tensor_scalar(row[:], idx_i[:, 0, :], 7, None, ALU.logical_shift_right))
                link(dve.tensor_copy(blk_b[:], row[:]))
                link(dve.tensor_scalar(row[:], idx_i[:, 0, :], P - 1, None, ALU.bitwise_and))
                dve.tensor_copy(rec[:, :, 0], row[:]).then_inc(rec_rdy, 1)
                def count(b):
                    link(dve.scalar_tensor_tensor(out=mask_b[:], in0=blk_b[:], scalar=iota_f[0:PS, ds(b, 1)],
                                                  in1=one_b[:], op0=ALU.is_equal, op1=ALU.mult,
                                                  accum_out=counts[:, ds(b, 1)]))
                link.loop(0, NB, 1, count)
                dve.sem_inc(cnt_rdy, 1)
                dve.wait_ge(pre_rdy, 1)
                link(dve.tensor_scalar(tot[:], ps_small[:, 1, 0:NB], float(GE - 1), None, ALU.add))
                link(dve.tensor_copy(n_groups_i[:], tot[:]))
                link(dve.tensor_scalar(n_groups_i[:], n_groups_i[:], 9, None, ALU.logical_shift_right))
                link(dve.tensor_copy(n_groups[:], n_groups_i[:]))
                link(dve.tensor_tensor_scan(end_group[:], ones[:, 0:NB], n_groups[:], 0.0, ALU.mult, ALU.add))
                link(dve.tensor_tensor(base[:], end_group[0:PS], n_groups[0:PS], ALU.subtract))
                link(dve.scalar_tensor_tensor(out=base[:], in0=base[:], scalar=float(GE), in1=ps_small[0:PS, 0, 0:NB],
                                              op0=ALU.mult, op1=ALU.add))
                def place(b):
                    for_b = base[:, ds(b, 1)]
                    link(dve.tensor_scalar(mask_b[:, t], blk_b[:, t], iota_f[0:PS, ds(b, 1)], None, ALU.is_equal))
                    link(dve.tensor_tensor_scan(cum[:, t], one_b[:, t], mask_b[:, t], for_b, ALU.mult, ALU.add))
                    link(dve.tensor_scalar(for_b, cum[:, t.stop - 1:t.stop], 1.0, None, ALU.mult))
                    link(dve.tensor_tensor(cum[:, t], cum[:, t], mask_b[:, t], ALU.mult))
                    link(dve.tensor_tensor(pos[:, t], pos[:, t], cum[:, t], ALU.add))
                for c in range(CH):
                    t = slice(c * EC, (c + 1) * EC)
                    link.loop(0, NB, 5, place)
                    link(dve.tensor_scalar(row[:, t], pos[:, t], -1.0, None, ALU.add))
                    if c == 0:
                        dve.wait_ge(rec_rdy, 3)
                    link.mark(dve.tensor_scalar(idx_i[:, 0, t], row[:, t], P - 1, None, ALU.bitwise_and))
                    link(dve.tensor_scalar(idx_i[:, 1, t], row[:, t], 7, None, ALU.logical_shift_right))
                    dve.scalar_tensor_tensor(out=row[:, t], in0=idx_i[:, 0, t], scalar=float(T1), in1=idx_i[:, 1, t],
                                             op0=ALU.mult, op1=ALU.add).then_inc(row_rdy, 1)
                    if c == 0:
                        dve.wait_ge(grp_ld, 160)
                        link(dve.tensor_copy(grp_f[:], grp_dst[:]))
                        dve.sem_inc(grp_rdy, 1)
                        link(dve.tensor_copy(grp_hi[:], grp_src[:]))
                        dve.sem_inc(grp_rdy, 1)
                        for i in range(2 * 4 * KT):
                            v, q, k = i // (4 * KT), i // KT % 4, i % KT
                            dve.wait_ge(tp_rdy, i + 1)
                            to = (dst_t, src_cols)[v]
                            dve.tensor_copy(to[:, q * GP:(q + 1) * GP, k], ps_t[:, i % 2, 0:GP]).then_inc(tp_used, 1)
                def group(b):
                    link(dve.scalar_tensor_tensor(out=gb[:], in0=iota_f[:, 0:NG], scalar=end_group[:, ds(b, 1)],
                                                  in1=gb[:], op0=ALU.is_ge, op1=ALU.add))
                link.loop(0, NB, 1, group)
                link.mark(dve.memset(group_block[:, 0:BLOCK_LEAD], 0))
                link(dve.tensor_scalar(group_block[:, BLOCK_LEAD:], gb[:], float(NB - 1), None, ALU.min))
                link(dve.tensor_scalar(sw_f[:], end_group[:, NB - 1:NB], float(UNROLL - 1), None, ALU.add))
                link(dve.tensor_copy(n_extra[:], sw_f[:]))
                link(dve.tensor_scalar(n_extra[:], n_extra[:], 3, None, ALU.logical_shift_right))
                link(dve.tensor_copy(sw_f[:], n_extra[:]))
                link(dve.tensor_scalar(n_extra[:], sw_f[:], -float(MIN_ROUNDS), None, ALU.add))
                link(dve.tensor_scalar(grp_dst[:], grp_dst[:], 7, None, ALU.logical_shift_right))
                link(dve.tensor_copy(grp_hi[:], grp_dst[:]))
                link(dve.tensor_reduce(lowest[:], grp_hi[:], AX, ALU.min))
                link(dve.scalar_tensor_tensor(out=grp_f[:], in0=grp_hi[:], scalar=float(NB), in1=grp_hi[:],
                                              op0=ALU.is_lt, op1=ALU.mult))
                link(dve.tensor_reduce(highest[:], grp_f[:], AX, ALU.max))
                link(dve.tensor_scalar(lowest[:], lowest[:], float(NB - 1), None, ALU.min))
                link(dve.tensor_tensor(highest[:], highest[:], lowest[:], ALU.subtract))
                link(dve.tensor_reduce(span[:], highest[:], AX, ALU.max))
                dve.sem_inc(lim_rdy, 1)
                link(dve.tensor_copy(dst_ti[:], dst_t[:]))
                link.mark(dve.tensor_scalar(rel_dst[:].bitcast(I32), dst_ti[:], P - 1, None, ALU.bitwise_and))
                link(dve.tensor_scalar(dst_ti[:], dst_ti[:], 7, None, ALU.logical_shift_right))
                link.mark(dve.tensor_copy(lo_t, rel_dst[:].bitcast(I32).rearrange("p g k -> p (g k)")))
                link(dve.tensor_copy(hi_t, dst_ti[:].rearrange("p g k -> p (g k)")))

                def hots(t, j):
                    wait(dve, hot_used, t - 7)
                    dve.tensor_scalar(lo_hot[:, j, :], iota_b[:, 0:P], lo_t[:, ds(t, 1)], None, ALU.is_equal)
                    dve.tensor_scalar(hi_hot[:, j, :], iota_b[:, 0:64], hi_t[:, ds(t, 1)], None, ALU.is_equal
                                      ).then_inc(hot_rdy, 1)
                for j in range(8):
                    hots(j, j)
                with loop(dve, 8, TD - 7, 8) as t0:
                    for j in range(8):
                        hots(t0 + j, j)
                dve.wait_ge(lim_t, 1)
                link.mark(dve.tensor_copy(win_f[:], ps_t[:, 0, 0:NGD]))
                link.mark(dve.tensor_copy(window0[:], ps_t[:, 0, 0:NGD]))
                link(dve.tensor_reduce(sw_f[:], ps_t[:, 1, 0:GP], AX, ALU.max))
                link(dve.tensor_copy(n_sweeps[:], sw_f[:]))
                link(dve.tensor_scalar(n_sweeps[:], n_sweeps[:], 1, None, ALU.logical_shift_right))
                link(dve.tensor_copy(sw_f[:], n_sweeps[:]))
                link(dve.tensor_scalar(n_sweeps[:], sw_f[:], 1.0, None, ALU.add))
                link(dve.scalar_tensor_tensor(out=rel_dst[:], in0=win_f[:].unsqueeze(2).broadcast_to([P, NGD, KT]),
                                              scalar=-float(P), in1=dst_t[:], op0=ALU.mult, op1=ALU.add))
                dve.wait_ge(hot_used, TD)
                link(dve.tensor_scalar(deg[:], ps_deg[:, 0:NB], 1.0, None, ALU.add))
                link(dve.tensor_copy(dis[:], deg[:]))

        tab = sb("tab", [P, NB, W])
        lo_e = sb("lo_e", [P, T1])
        typ_e = sb("typ_e", [P, T1])
        dst_e = sb("dst_e", [P, T1], I32)

        with ExitStack() as ph:
            def sb2(name, shape, dt=F32):
                return ph.enter_context(nc.sbuf_tensor(name, shape, dt))

            def sem2(name):
                return ph.enter_context(nc.semaphore(name))

            g_sb = sb2("g_sb", [C, 2, 3, C])
            b_sb = sb2("b_sb", [C, 2, 3, C])
            h0 = sb2("h0", [C, C])
            rz = sb2("rz", [C, 2, C])
            nn = sb2("nn", [C, C])
            tmp = sb2("tmp", [C, C])
            fcw = sb2("fcw", [C, 2 * C])
            fcb = sb2("fcb", [C, 1])
            rel = sb2("rel", [C, R])
            rec_e = sb2("rec_e", [P, T1, 4], I32)
            ps_p = ph.enter_context(nc.psum_tensor("ps_p", [P, 3, 128], F32))
            rec_ld = sem2("rec_ld")
            ld2, fc_ld, dv2, s_rdy, rz_rdy, n_rdy, t_rdy, p_rdy, sq_rdy = map(
                sem2, ("ld2", "fc_ld", "dv2", "s_rdy", "rz_rdy", "n_rdy", "t_rdy", "p_rdy", "sq_rdy"))
            block = ph.enter_context(nc.Block())

            @block.sync
            def _(sp):
                sp.dma_start(rec_e[:].rearrange("p t f -> p (t f)"), rec_d.rearrange("(p t) f -> p (t f)", p=P)
                             ).then_inc(rec_ld, 16)
                sp.dma_start(fcw[:], fc_w).then_inc(fc_ld, 16)
                sp.dma_start(fcb[:], fc_b).then_inc(fc_ld, 16)
                sp.dma_start(rel[:], relT).then_inc(fc_ld, 16)
                gv = gate_d.rearrange("(m k) c -> m (k c)", m=2).rearrange("m (t i o) -> m t i o", t=3, o=C)
                for m, b in enumerate((b_ih, b_hh)):
                    for t in range(3):
                        sp.dma_start(g_sb[:, m, t, :], gv[m, t]).then_inc(ld2, 16)
                    sp.dma_start(b_sb[:, m], b.rearrange("(t i o) -> i t o", t=3, o=C)).then_inc(ld2, 16)
                sp.dma_start(h0[:], h_mat).then_inc(ld2, 16)

            @block.tensor
            def _(pe):
                pe.wait_ge(fc_ld, 48)
                pe.matmul(ps_p[0:C, 0, 0:R], lhsT=fcw[:, 0:C], rhs=rel[:], start=True, stop=True)
                pe.matmul(ps_p[0:C, 1, 0:R], lhsT=fcw[:, C:2 * C], rhs=rel[:], start=True, stop=True)
                pe.matmul(ps_p[C:C + 1, 2, 0:R], lhsT=fcb[:], rhs=rel[:], start=True, stop=True).then_inc(p_rdy, 1)

            @block.vector
            def _(dve):
                link = Chain(dve, dv2)
                dve.wait_ge(p_rdy, 1)
                link(dve.memset(p12[:], 0.0))
                link.mark(dve.tensor_copy(p12[0:C, 0:R], ps_p[0:C, 0, 0:R]))
                link.mark(dve.tensor_copy(p12[0:C, R:2 * R], ps_p[0:C, 1, 0:R]))
                link.mark(dve.tensor_copy(p12[C:C + 1, R:2 * R], ps_p[C:C + 1, 2, 0:R]))
                dve.wait_ge(sq_rdy, 1)
                link(dve.reciprocal(dis[:], dis[:]))
                dve.wait_ge(ld2, 9 * 16)
                link(dve.tensor_tensor(g_sb[:], g_sb[:], b_sb[:], ALU.add))
                dve.tensor_tensor(rz[:], g_sb[:, 0, 0:2, :], g_sb[:, 1, 0:2, :], ALU.add).then_inc(s_rdy, 1)
                dve.wait_ge(rz_rdy, 1)
                link(dve.tensor_tensor(nn[:], rz[:, 0, :], g_sb[:, 1, 2, :], ALU.mult))
                dve.tensor_tensor(nn[:], nn[:], g_sb[:, 0, 2, :], ALU.add).then_inc(n_rdy, 1)
                dve.wait_ge(t_rdy, 1)
                link(dve.tensor_tensor(tmp[:], h0[:], nn[:], ALU.subtract))
                link(dve.tensor_tensor(tmp[:], tmp[:], rz[:, 1, :], ALU.mult))
                link(dve.memset(weight[:], 0.0))
                link(dve.tensor_tensor(weight[0:C, :], tmp[:], nn[:], ALU.add))
                dve.wait_ge(rec_ld, 16)
                link(dve.tensor_copy(lo_e[:], rec_e[:, :, 0]))
                link(dve.tensor_copy(dst_e[:], rec_e[:, :, 1]))
                link(dve.tensor_copy(typ_e[:], rec_e[:, :, 2]))
                link(dve.memset(tab[:], 0.0))
                link(dve.tensor_copy(tab[:, :, 0:C], x0[:]))
                link(dve.memset(tab[:, :, ONE:ONE + 1], 1.0))

            @block.scalar
            def _(act):
                act.activation(dis[:], dis[:], ACT.Sqrt).then_inc(sq_rdy, 1)
                act.wait_ge(s_rdy, 1)
                act.activation(rz[:], rz[:], ACT.Sigmoid).then_inc(rz_rdy, 1)
                act.wait_ge(n_rdy, 1)
                act.activation(nn[:], nn[:], ACT.Tanh).then_inc(t_rdy, 1)

        def project(pe, dve, link, rhs, cols, take, s):
            in_rdy, tt_rdy, tt_cp, pr_rdy, pr_cp, ps_e, ps_a, seven, turned = s
            assert NB % 7 == 0

            def pe_part(b7):
                pe.wait_ge(in_rdy, b7 + 1)
                for j in range(7):
                    mm = pe.transpose(ps_e[:, j, :], seven[:, j, :], ident_f[:])
                mm.then_inc(tt_rdy, 1)
                pe.wait_ge(tt_cp, b7 + 1)
                for j in range(7):
                    mm = pe.matmul(ps_a[:, j, 0:cols], lhsT=turned[:, j, :], rhs=rhs[:, 0:cols], start=True, stop=True)
                mm.then_inc(pr_rdy, 1)

            if pe is not None:
                pe_part(0)
                with loop(pe, 1, NB // 7) as b7:
                    pe.wait_ge(pr_cp, b7)
                    pe_part(b7)
            else:
                def dve_part(b7):
                    dve.tensor_scalar(seven[:], tab[:, ds(b7 * 7, 7), :], 1.0, None, ALU.mult).then_inc(in_rdy, 1)
                    dve.wait_ge(tt_rdy, b7 + 1)
                    dve.tensor_copy(turned[:], ps_e[:, 0:7, :]).then_inc(tt_cp, 1)
                    dve.wait_ge(pr_rdy, b7 + 1)
                    take(b7).then_inc(pr_cp, 1)
                with loop(dve, 0, NB // 7) as b7:
                    dve_part(b7)

        for hop in range(2):
            with ExitStack() as ph:
                def sbh(name, shape, dt=F32):
                    return ph.enter_context(nc.sbuf_tensor(f"{name}_{hop}", shape, dt))

                def psh(name, shape, dt=F32):
                    return ph.enter_context(nc.psum_tensor(f"{name}_{hop}", shape, dt))

                def semh(name):
                    return ph.enter_context(nc.semaphore(f"{name}_{hop}"))

                acc = sbh("acc", [P, NB, C + 1])
                m_run = sbh("m_run", [P, NB])
                a_split = sbh("a_split", [P, NB, 3, R], BF16)
                st = ph.enter_context(ExitStack())
                a_all = st.enter_context(nc.sbuf_tensor(f"a_all_{hop}", [P, NB, 2 * R], F32))
                seven = st.enter_context(nc.sbuf_tensor(f"seven_{hop}", [P, 7, P], F32))
                turned = st.enter_context(nc.sbuf_tensor(f"turned_{hop}", [P, 7, P], F32))
                ps_e = st.enter_context(nc.psum_tensor(f"ps_e_{hop}", [P, 8, P], F32))
                ps_a = st.enter_context(nc.psum_tensor(f"ps_a_{hop}", [P, 8, P], F32))
                names = ("in_rdy", "tt_rdy", "tt_cp", "pr_rdy", "pr_cp")
                s = (*map(semh, names), ps_e, ps_a, seven, turned)
                tab_rdy, tab_st, dvt = semh("tab_rdy"), semh("tab_st"), semh("dvt")
                with nc.Block() as block:
                    @block.tensor
                    def _(pe):
                        project(pe, None, None, p12, 2 * R, None, s)

                    @block.vector
                    def _(dve):
                        link = Chain(dve, dvt)
                        dve.memset(acc[:], 0.0)
                        dve.memset(m_run[:], NO_SCORE)
                        project(None, dve, link, p12, 2 * R, lambda b7: dve.tensor_scalar(
                            a_all[:, ds(b7 * 7, 7), :], ps_a[:, 0:7, 0:2 * R], 1.0, None, ALU.mult), s)
                        dve.wait_ge(s[4], NB // 7)
                        dve.tensor_copy(tab[:, :, SC:SC + R], a_all[:, :, R:2 * R]).then_inc(tab_rdy, 1)
                        for j in range(3):
                            link(dve.tensor_copy(a_split[:, :, j, :], a_all[:, :, 0:R]))
                            if j < 2:
                                link(dve.tensor_tensor(a_all[:, :, 0:R], a_all[:, :, 0:R], a_split[:, :, j, :],
                                                       ALU.subtract))

                    @block.sync
                    def _(sp):
                        sp.wait_ge(tab_rdy, 1)
                        sp.dma_start(tab_d[hop].rearrange("(b p) w -> p b w", p=P), tab[:]).then_inc(tab_st, 16)
                        sp.wait_ge(tab_st, 16)
                st.close()

                stage_idx = sbh("stage_idx", [P, 2, 16], I32)
                rows = sbh("rows", [P, 8, KT, W])
                hot = sbh("hot", [P, 2, KT, P], BF16)
                hot_t = sbh("hot_t", [P, 2, GE], BF16)
                lower = sbh("lower", [P, 2, GE], BF16)
                picked = sbh("picked", [P, KT, R])
                s_raw = sbh("s_raw", [P, 2, KT])
                score = sbh("score", [P, 2, KT])
                masked = sbh("masked", [P, 2, GE])
                m_group = sbh("m_group", [P, 2])
                m_new = sbh("m_new", [P, 2])
                m_neg = sbh("m_neg", [P, 2])
                m_diff = sbh("m_diff", [P, 2, 2])
                alpha = sbh("alpha", [P, 2, 2])
                prob_t = sbh("prob_t", [P, 2, GE])
                prob = sbh("prob", [P, 2, GE])
                kept = sbh("kept", [P, 2, C + 1])
                inv = sbh("inv", [P, NB])
                sq = sbh("sq", [P, NB, C])
                ps_hot = psh("ps_hot", [P, 2 * GE], BF16)
                ps_x = psh("ps_x", [P, 2, 512])
                ps_s = psh("ps_s", [P, 2, GE])
                ps_p = psh("ps_p", [P, GE])
                ps_g = psh("ps_g", [P, 2, 512])
                (hot_rdy, hot_turned, hot_t_rdy, lower_rdy, x_rdy, score_rdy, s_spread, masked_rdy, exp_rdy, p_turned,
                 prob_rdy, summed, added, staged, tick, dvh, norm_sq, norm_rdy) = map(semh, (
                     "hot_rdy", "hot_turned", "hot_t_rdy", "lower_rdy", "x_rdy", "score_rdy", "s_spread", "masked_rdy",
                     "exp_rdy", "p_turned", "prob_rdy", "summed", "added", "staged", "tick", "dvh", "norm_sq",
                     "norm_rdy"))
                dtick = semh("dtick")
                landed = [semh(f"landed{i}") for i in range(8)]
                def live(eng):
                    return eng.value_load(n_extra[0:1, 0:1], min_val=0, max_val=NG // UNROLL - MIN_ROUNDS) + MIN_ROUNDS

                with nc.Block() as block:
                    @block.gpsimd
                    def _(pool):
                        def half(it, h):
                            g0 = it * 8 + h * 4
                            for g in range(4):
                                wait(pool, landed[h * 4 + g], it * 64)
                            wait_pool(pool, tick, summed, g0 - 7)
                            pool.tensor_copy(stage_idx[:, h, :], dst_e[:, ds(g0 * KT, 16)]).then_inc(staged, 1)
                            wait_pool(pool, tick, staged, it * 2 + h + 1)
                            for g in range(4):
                                if g:
                                    wait_pool(pool, tick, summed, g0 + g - 7)
                                for k in range(KT):
                                    j = g * KT + k
                                    pool.indirect_dma_start(
                                        out=rows[:, h * 4 + g, k, :], out_offset=None, in_=tab_d[hop],
                                        in_offset=bass.IndirectOffsetOnAxis(ap=stage_idx[:, h, j:j + 1], axis=0)
                                    ).then_inc(landed[h * 4 + g], 16)
                        pool_n = live(pool)
                        for h in range(2):
                            half(0, h)
                        with loop(pool, 1, pool_n) as it:
                            for h in range(2):
                                half(it, h)

                    @block.tensor
                    def _(pe):
                        def spread(g, p):
                            wait(pe, score_rdy, g + 1)
                            wait(pe, masked_rdy, g - 1)
                            for k in range(KT):
                                mm = pe.transpose(ps_s[:, p, k * P:(k + 1) * P],
                                                  score[:, p, k:k + 1].broadcast_to([P, P]), ident_f[:])
                            mm.then_inc(s_spread, 1)

                        def turn_prob(g, p):
                            wait(pe, exp_rdy, g + 1)
                            wait(pe, prob_rdy, g)
                            for k in range(KT):
                                mm = pe.transpose(ps_p[:, k * P:(k + 1) * P], prob_t[:, p, k * P:(k + 1) * P],
                                                  ident_f[:])
                            mm.then_inc(p_turned, 1)

                        def turn_hot(g, p):
                            wait(pe, hot_rdy, g + 1)
                            wait(pe, lower_rdy, g)
                            for k in range(KT):
                                mm = pe.transpose(ps_hot[:, k * P:(k + 1) * P], hot[:, p, k, :], ident_b[:])
                            mm.then_inc(hot_turned, 1)

                        def scores(g, p, u, bb):
                            wait(pe, landed[u], (g - u) * 8 + 64)
                            wait(pe, hot_t_rdy, g + 1)
                            wait(pe, score_rdy, g - 1)
                            for k in range(KT):
                                for j in range(3):
                                    pe.matmul(ps_x[:, p, k * R:(k + 1) * R], lhsT=hot_t[:, p, k * P:(k + 1) * P],
                                              rhs=a_split[:, ds(bb, 1), j, :].rearrange("p a r -> p (a r)"),
                                              start=(k == 0 and j == 0), stop=False, skip_group_check=True)
                            mm = pe.matmul(ps_x[:, p, 0:KT * R], lhsT=ident_f[:], rhs=rows[:, u, :, SC:SC + R],
                                           start=False, stop=True, skip_group_check=True)
                            mm.then_inc(x_rdy, 1)

                        def sums(g, p, u):
                            wait(pe, prob_rdy, g + 1)
                            wait(pe, added, g - 1)
                            for k in range(KT):
                                mm = pe.matmul(ps_g[:, p, 0:C + 1], lhsT=prob[:, p, k * P:(k + 1) * P],
                                               rhs=rows[:, u, k, 0:C + 1], start=(k == 0), stop=(k == KT - 1))
                            mm.then_inc(summed, 1)

                        def body(i, u, stages, block_of):
                            _, a, b, c = stages
                            if a:
                                turn_hot(i - 1, (u - 1) % 2)
                            if b:
                                spread(i - 2, u % 2)
                            if c:
                                turn_prob(i - 3, (u - 3) % 2)
                            if a:
                                scores(i - 1, (u - 1) % 2, (u - 1) % 8, block_of(1))
                            if c:
                                sums(i - 3, (u - 3) % 2, (u - 3) % 8)
                        pipelined(pe, live(pe) * UNROLL, body, group_block, NB - 1)

                    @block.scalar
                    def _(act):
                        def body(i, u, stages, _):
                            _, a, b, c = stages
                            p = (u - 1) % 2
                            if a:
                                g = i - 1
                                wait(act, hot_turned, g + 1)
                                wait(act, x_rdy, g - 1)
                                act.activation(hot_t[:, p, :], ps_hot[:, 0:GE], ACT.Copy).then_inc(hot_t_rdy, 1)
                                wait(act, masked_rdy, g - 1)
                                act.activation(lower[:, p, :], ps_hot[:, 0:GE], ACT.Copy, bias=-BIG, scale=BIG
                                               ).then_inc(lower_rdy, 1)
                            if c:
                                g = i - 3
                                wait(act, p_turned, g + 1)
                                wait(act, summed, g - 1)
                                act.activation(prob[:, p, :], ps_p[:], ACT.Copy).then_inc(prob_rdy, 1)
                            if b:
                                g, q = i - 2, 1 - p
                                wait(act, masked_rdy, g + 1)
                                wait(act, p_turned, g - 1)
                                act.activation(prob_t[:, q, :], masked[:, q, :], ACT.Exp, bias=m_neg[:, q:q + 1])
                                wait(act, added, g - 1)
                                act.activation(alpha[:, q, :], m_diff[:, q, :], ACT.Exp).then_inc(exp_rdy, 1)
                        pipelined(act, live(act) * UNROLL, body)
                        act.wait_ge(norm_sq, 1)
                        act.activation(inv[:], inv[:], ACT.Sqrt).then_inc(norm_rdy, 1)

                    @block.vector
                    def _(dve):
                        link = Chain(dve, dvh)

                        def body(i, u, stages, block_of):
                            z, a, b, c = stages
                            if b:
                                g, p = i - 2, u % 2
                                bb = block_of(2)
                                wait(dve, lower_rdy, g + 1)
                                wait(dve, exp_rdy, g - 1)
                                wait(dve, s_spread, g + 1)
                                dve.sem_inc(dtick, 1)
                                link.mark(dve.tensor_tensor_reduce(masked[:, p, :], lower[:, p, :], ps_s[:, p, :], 1.0,
                                                                   -3e38, ALU.add, ALU.max, m_group[:, p:p + 1]))

                            def one_hot(k, last=False):
                                if z:
                                    ins = dve.tensor_scalar(hot[:, u % 2, k, :], iota_b[:, 0:P],
                                                            lo_e[:, ds(i * KT + k, 1)], None, ALU.is_equal)
                                    if last:
                                        ins.then_inc(hot_rdy, 1)
                            if z:
                                wait(dve, hot_turned, i - 1)
                            one_hot(0)
                            one_hot(1)
                            if b:
                                link.sync()
                                link.mark(dve.tensor_tensor(m_new[:, p:p + 1], m_run[:, ds(bb, 1)], m_group[:, p:p + 1],
                                                            ALU.max))
                            one_hot(2)
                            if b:
                                link.sync()
                                dve.tensor_tensor(m_diff[:, p, 0:1], m_run[:, ds(bb, 1)], m_new[:, p:p + 1], ALU.subtract)
                                dve.tensor_tensor(m_diff[:, p, 1:2], m_group[:, p:p + 1], m_new[:, p:p + 1], ALU.subtract)
                                dve.tensor_scalar(m_neg[:, p:p + 1], m_group[:, p:p + 1], -1.0, None, ALU.mult
                                                  ).then_inc(masked_rdy, 1)
                            one_hot(3, last=True)
                            if b:
                                wait(dve, masked_rdy, g + 1)
                                link.mark(dve.tensor_scalar(m_run[:, ds(bb, 1)], m_new[:, p:p + 1], 1.0, None, ALU.mult))
                            if a:
                                g, q = i - 1, (u - 1) % 2
                                wait(dve, x_rdy, g + 1)
                                for k in range(KT):
                                    ins = dve.scalar_tensor_tensor(
                                        out=picked[:, k, :], in0=iota_f[:, 0:R], scalar=typ_e[:, ds(g * KT + k, 1)],
                                        in1=ps_x[:, q, k * R:(k + 1) * R], op0=ALU.is_equal, op1=ALU.mult,
                                        accum_out=s_raw[:, q, k:k + 1])
                                    link.mark(ins)
                                wait(dve, s_spread, g - 1)
                                link.sync()
                                dve.scalar_tensor_tensor(out=score[:, q, :], in0=s_raw[:, q, :], scalar=0.2,
                                                         in1=s_raw[:, q, :], op0=ALU.mult, op1=ALU.max
                                                         ).then_inc(score_rdy, 1)
                            if c:
                                g, q = i - 3, (u - 3) % 2
                                sums_of = acc[:, ds(block_of(3), 1), :].rearrange("p a c -> p (a c)")
                                wait(dve, summed, g + 1)
                                wait(dve, added, g)
                                link(dve.tensor_scalar(kept[:, q, :], sums_of, alpha[:, q, 0:1], None, ALU.mult))
                                dve.scalar_tensor_tensor(out=sums_of, in0=ps_g[:, q, 0:C + 1], scalar=alpha[:, q, 1:2],
                                                         in1=kept[:, q, :], op0=ALU.mult, op1=ALU.add
                                                         ).then_inc(added, 1)
                        n = live(dve) * UNROLL
                        pipelined(dve, n, body, group_block, NB - 1, link)
                        emb = tab[:, :, 0:C]
                        dve.wait_ge(added, n)
                        link(dve.tensor_scalar(inv[:], acc[:, :, C], 0.5, None, ALU.max))
                        link(dve.reciprocal(inv[:], inv[:]))
                        link(dve.tensor_tensor(sq[:], acc[:, :, 0:C], inv[:].unsqueeze(2).broadcast_to([P, NB, C]), ALU.mult))
                        link(dve.tensor_tensor(emb, emb, sq[:], ALU.add))
                        link(dve.tensor_tensor(sq[:], emb, emb, ALU.mult))
                        link(dve.tensor_reduce(inv[:], sq[:], AX, ALU.add))
                        dve.tensor_scalar(inv[:], inv[:], 1e-24, None, ALU.max).then_inc(norm_sq, 1)
                        dve.wait_ge(norm_rdy, 1)
                        link(dve.reciprocal(inv[:], inv[:]))
                        link(dve.tensor_tensor(emb, emb, inv[:].unsqueeze(2).broadcast_to([P, NB, C]), ALU.mult))
                        dve.sem_inc(dtick, 1)

        with ExitStack() as ph:
            def sbl(name, shape, dt=F32):
                return ph.enter_context(nc.sbuf_tensor(name, shape, dt))

            def psl(name, shape, dt=F32):
                return ph.enter_context(nc.psum_tensor(name, shape, dt))

            def seml(name):
                return ph.enter_context(nc.semaphore(name))

            y = sbl("y", [P, NB, C])
            total = sbl("total", [P, AB, C])
            cen = sbl("cen", [P, NB, C])
            ssq = sbl("ssq", [P, NB, C])
            mean = sbl("mean", [P, NB])
            var = sbl("var", [P, NB])
            eps = sbl("eps", [P, 1])
            seven = sbl("seven", [P, 7, P])
            turned = sbl("turned", [P, 7, P])
            rows = sbl("y_rows", [P, 4, KT, C])
            stage_idx = sbl("stage_src", [P, 2, 16], I32)
            near = sbl("near", [P, 2, KT, 2 * P])
            var_rdy, sd_rdy = seml("var_rdy"), seml("sd_rdy")

            def layernorm(dve, link, n):
                link(dve.tensor_reduce(mean[:], x0[:], AX, ALU.add))
                link(dve.tensor_scalar(mean[:], mean[:], 1.0 / C, None, ALU.mult))
                link(dve.tensor_tensor(cen[:], x0[:], mean[:].unsqueeze(2).broadcast_to([P, NB, C]), ALU.subtract))
                link(dve.tensor_tensor(ssq[:], cen[:], cen[:], ALU.mult))
                link(dve.tensor_reduce(var[:], ssq[:], AX, ALU.add))
                dve.tensor_scalar(var[:], var[:], 1.0 / C, 1e-5, ALU.mult, ALU.add).then_inc(var_rdy, 1)
                dve.wait_ge(sd_rdy, n)
                link(dve.reciprocal(var[:], var[:]))
                link(dve.tensor_tensor(x0[:], cen[:], var[:].unsqueeze(2).broadcast_to([P, NB, C]), ALU.mult))

            def root(act, n):
                act.wait_ge(var_rdy, n)
                act.activation(var[:], var[:], ACT.Sqrt).then_inc(sd_rdy, 1)

            with ExitStack() as st:
                ps_e = st.enter_context(nc.psum_tensor("ps_e_y", [P, 8, P], F32))
                ps_a = st.enter_context(nc.psum_tensor("ps_a_y", [P, 8, P], F32))
                s = (*map(seml, ("in_rdy_y", "tt_rdy_y", "tt_cp_y", "pr_rdy_y", "pr_cp_y")), ps_e, ps_a, seven, turned)
                x_set, y_rdy, y_st, dvy = map(seml, ("x_set", "y_rdy", "y_st", "dvy"))
                with nc.Block() as block:
                    @block.vector
                    def _(dve):
                        link = Chain(dve, dvy)
                        dve.memset(total[:], 0.0)
                        link(dve.tensor_tensor(x0[:], x0[:], tab[:, :, 0:C], ALU.add))
                        layernorm(dve, link, 1)
                        dve.tensor_copy(tab[:, :, 0:C], x0[:]).then_inc(x_set, 1)
                        dve.wait_ge(x_set, 1)
                        project(None, dve, link, weight, C, lambda b7: dve.tensor_scalar(
                            y[:, ds(b7 * 7, 7), :], ps_a[:, 0:7, 0:C], 1.0, None, ALU.mult), s)
                        dve.wait_ge(s[4], NB // 7)
                        link(dve.tensor_tensor(y[:], y[:], dis[:].unsqueeze(2).broadcast_to([P, NB, C]), ALU.mult))
                        dve.sem_inc(y_rdy, 1)

                    @block.scalar
                    def _(act):
                        root(act, 1)

                    @block.tensor
                    def _(pe):
                        pe.wait_ge(x_set, 1)
                        project(pe, None, None, weight, C, None, s)

                    @block.sync
                    def _(sp):
                        sp.wait_ge(y_rdy, 1)
                        sp.dma_start(y_d.rearrange("(b p) w -> p b w", p=P), y[:]).then_inc(y_st, 16)
                        sp.wait_ge(y_st, 16)

            ps_g = psl("ps_gy", [P, 2, 512])
            near_rdy, summed, added, staged, tick, dvl, fin_rdy, out_st = map(seml, (
                "near_rdy", "summed_y", "added_y", "staged_y", "tick_y", "dvl", "fin_rdy", "out_st"))
            landed = [seml(f"landed_y{i}") for i in range(4)]
            dtick_l = seml("dtick_l")
            AHEAD = 4
            with nc.Block() as block:
                @block.gpsimd
                def _(pool):
                    sweeps = pool.value_load(n_sweeps[0:1, 0:1], min_val=1, max_val=NB // 2 + 1)
                    with loop(pool, 0, sweeps) as w:
                        with loop(pool, 0, NGD // 8) as it:
                            for h in range(2):
                                f0 = w * NGD + it * 8 + h * 4
                                wait_pool(pool, tick, summed, f0 - 3 + AHEAD)
                                pool.tensor_copy(stage_idx[:, h, :], src_cols[:, ds(it * 8 + h * 4, 4), :]
                                                 .rearrange("p g k -> p (g k)")).then_inc(staged, 1)
                                wait_pool(pool, tick, staged, w * (NGD // 4) + it * 2 + h + 1)
                                for g in range(4):
                                    if g:
                                        wait_pool(pool, tick, summed, f0 + g - 3 + AHEAD)
                                    for k in range(KT):
                                        j = g * KT + k
                                        pool.indirect_dma_start(
                                            out=rows[:, g, k, :], out_offset=None, in_=y_d,
                                            in_offset=bass.IndirectOffsetOnAxis(ap=stage_idx[:, h, j:j + 1], axis=0)
                                        ).then_inc(landed[g], 16)

                @block.tensor
                def _(pe):
                    pe.sem_inc(summed, AHEAD)
                    sweeps = pe.value_load(n_sweeps[0:1, 0:1], min_val=1, max_val=NB // 2 + 1)
                    with loop(pe, 0, sweeps) as w:
                        with loop(pe, 0, NGD - 3, 4) as i0:
                            for u in range(4):
                                f = w * NGD + i0 + u
                                pe.wait_ge(landed[u], (w * NGD + i0) * 16 + 64)
                                pe.wait_ge(near_rdy, f + 1)
                                pe.wait_ge(added, f - 1 + AHEAD)
                                for j in range(2):
                                    for k in range(KT):
                                        mm = pe.matmul(ps_g[:, u % 2, j * C:(j + 1) * C], lhsT=near[:, u % 2, k, j * P:(j + 1) * P],
                                                       rhs=rows[:, u, k, :], start=(k == 0), stop=(k == KT - 1))
                                mm.then_inc(summed, 1)

                @block.vector
                def _(dve):
                    link = Chain(dve, dvl)
                    dve.sem_inc(added, AHEAD)
                    sweeps = dve.value_load(n_sweeps[0:1, 0:1], min_val=1, max_val=NB // 2 + 1)

                    def windows(i, f, u):
                        dve.wait_ge(summed, f - 1 + AHEAD)
                        for k in range(KT):
                            ins = dve.tensor_scalar(near[:, u % 2, k, :], iota_f[:, 0:2 * P], rel_dst[:, ds(i, 1), k],
                                                    None, ALU.is_equal)
                        ins.then_inc(near_rdy, 1)

                    def add(i, f, w, u):
                        first = dve.value_load(window0[0:1, ds(i, 1)], min_val=0, max_val=NB - 1)
                        t = total[:, ds(first + w * 2, 2), :]
                        dve.wait_ge(summed, f + 1 + AHEAD)
                        dve.wait_ge(added, f + AHEAD)
                        dve.tensor_tensor(t, t, ps_g[:, u % 2, 0:2 * C].rearrange("p (j c) -> p j c", j=2), ALU.add).then_inc(added, 1)

                    with loop(dve, 0, sweeps) as w:
                        f0 = w * NGD
                        windows(0, f0, 0)
                        for u in range(1, 4):
                            windows(u, f0 + u, u)
                            add(u - 1, f0 + u - 1, w, u - 1)
                        with loop(dve, 4, NGD - 3, 4) as i0:
                            for u in range(4):
                                windows(i0 + u, f0 + i0 + u, u)
                                add(i0 + u - 1, f0 + i0 + (u - 1), w, u - 1)
                        add(NGD - 1, f0 + NGD - 1, w, 3)
                        dve.tensor_scalar(rel_dst[:], rel_dst[:], -2.0 * P, None, ALU.add).then_inc(dvl, 1)
                        dve.wait_ge(dvl, w + 1)
                        dve.sem_inc(dtick_l, 1)

                    link.base = sweeps
                    link(dve.tensor_tensor(y[:], y[:], total[:, 0:NB, :], ALU.add))
                    link(dve.tensor_tensor(y[:], y[:], dis[:].unsqueeze(2).broadcast_to([P, NB, C]), ALU.mult))
                    link(dve.tensor_scalar(y[:], y[:], 0.0, None, ALU.max))
                    link(dve.tensor_tensor(x0[:], x0[:], y[:], ALU.add))
                    layernorm(dve, link, 2)
                    dve.sem_inc(fin_rdy, 1)

                @block.scalar
                def _(act):
                    root(act, 2)

                @block.sync
                def _(sp):
                    sp.wait_ge(fin_rdy, 1)
                    sp.dma_start(out[0:FULL * P].rearrange("(b p) c -> p b c", p=P), x0[:, 0:FULL, :]).then_inc(out_st, 16)
                    sp.dma_start(out[FULL * P:N], x0[0:REST, FULL, :]).then_inc(out_st, 16)
                    sp.wait_ge(out_st, 32)


def kernel(**inputs):
    import numpy as np
    import concourse.bacc as bacc
    from concourse.bass_utils import run_bass_kernel_spmd

    def turned(w):
        r, k = w.shape
        return np.ascontiguousarray(w.reshape(r // 512, 512, k // 512, 4, 128).transpose(0, 2, 4, 3, 1))

    a = {k: np.asarray(v) for k, v in inputs.items()}
    arrays = {
        "x": a["x"], "src": a["src"], "dst": a["dst"], "typ": a["edge_type_50"],
        "relT": np.ascontiguousarray(a["L0_gnn_relation_emb"].T),
        "fc_w": a["L0_gnn_fc_w"], "fc_b": np.ascontiguousarray(a["L0_gnn_fc_b"][:, None]),
        "w_ih": turned(a["L1_gnn_w_ih"]), "w_hh": turned(a["L1_gnn_w_hh"]),
        "h_col": np.ascontiguousarray(a["L1_gnn_initial_weight"].reshape(-1, 128).T),
        "h_mat": a["L1_gnn_initial_weight"],
        "b_ih": a["L1_gnn_b_ih"], "b_hh": a["L1_gnn_b_hh"],
    }
    nc = bacc.Bacc("TRN2", target_bir_lowering=False, num_devices=1)
    args = [nc.dram_tensor(k, v.shape, mybir.dt.from_np(v.dtype), kind="ExternalInput").ap() for k, v in arrays.items()]
    out = nc.dram_tensor("out", a["x"].shape, F32, kind="ExternalOutput").ap()
    gnn_kernel(nc, *args, out)
    r = run_bass_kernel_spmd(nc, [arrays], core_ids=[0])
    return r.results[0]["out"]
```

```python
from contextlib import ExitStack

import concourse.bass as bass
from concourse import mybir

ALU = mybir.AluOpType
ACT = mybir.ActivationFunctionType
AX = mybir.AxisListType.X
F32 = mybir.dt.float32
BF16 = mybir.dt.bfloat16
I32 = mybir.dt.int32

P = 128
NODES = 125
BIG = float(2.0 ** 100)
NO_SCORE = -float(2.0 ** 97)
PAD_DST = 30000
PAD_LO = 200
KT = 4
GE = KT * P


def ds(start, n):
    return bass.ds(start, n)


def loop(eng, lo, hi, step=1):
    return eng.bass.Fori(lo, hi, step, engines=(eng.engine,), hint_back_edge=True)


def wait(eng, sem, value):
    if isinstance(value, int) and value <= 0:
        return
    eng.wait_ge(sem, value)


def wait_pool(pool, tick, sem, value):
    if isinstance(value, int) and value <= 0:
        return
    pool.wait_ge(sem, value)
    pool.sem_inc(tick, 1)


class Chain:

    def __init__(self, eng, sem, tick=None):
        self.eng, self.sem, self.tick, self.base, self.n = eng, sem, tick, 0, 0

    def __call__(self, ins):
        self.n += 1
        ins.then_inc(self.sem, 1)
        self.eng.wait_ge(self.sem, self.base + self.n)

    def mark(self, ins):
        self.n += 1
        ins.then_inc(self.sem, 1)

    def sync(self):
        self.eng.wait_ge(self.sem, self.base + self.n)

    def loop(self, hi, step, per, body):
        assert hi % step == 0
        before = self.base + self.n
        with loop(self.eng, 0, hi - step + 1, step) as i0:
            self.base, self.n = i0 * per + before, 0
            body(i0, step)
            self.eng.sem_inc(self.tick, 1)
            assert self.n == per * step, (self.n, per)
        self.base, self.n = before + hi * per, 0


BLOCK_BACK = 4


def blocks_from(eng, table, i0, n, top):
    _, v = eng.bass.values_load_multi_w_load_instructions(
        table[0:1, ds(i0 + BLOCK_LEAD - BLOCK_BACK, n + BLOCK_BACK)], engines=(eng.engine,), min_val=0, max_val=top,
        skip_runtime_bounds_check_because="the table is held below the number of blocks")
    return v


BLOCK_LEAD = 8
LAG = 3
UNROLL = 8


def pipelined(eng, n, body, table=None, top=0, link=None):
    def steps(i0, count, flags):
        v = blocks_from(eng, table, i0, UNROLL if count == UNROLL else 0, top) if table is not None else None
        for u in range(count):
            body(i0 + u, u, flags(u), (lambda d, u=u: v[BLOCK_BACK + u - d]))

    steps(0, UNROLL, lambda u: (True, u >= 1, u >= 2, u >= 3))
    before = link.base + link.n if link else 0
    with loop(eng, UNROLL, n - UNROLL + 1, UNROLL) as i0:
        if link:
            link.base, link.n = (i0 - UNROLL) * PER_GROUP + before, 0
        steps(i0, UNROLL, lambda u: (True,) * 4)
        assert not link or link.n == PER_GROUP * UNROLL, link.n
    if link:
        link.base, link.n = (n - UNROLL) * PER_GROUP + before, 0
    steps(n, LAG, lambda u: (False, u < 1, u < 2, True))


PER_GROUP = 8


def gnn_kernel(nc, x, src, dst, typ, relT, fc_w, fc_b, w_ih, w_hh, h_col, h_mat, b_ih, b_hh, out):
    N, C = x.shape
    E = src.shape[0]
    R = relT.shape[1]
    NB = N // NODES
    assert NB * NODES == N and NODES <= P and NB % 10 == 0 and NB <= 64
    PS = 125
    ES = E // PS
    CUTS = [0, ES * 2 // 25, ES * 6 // 25, ES * 11 // 25, ES * 18 // 25, ES]
    HIDDEN = ES * 23 // 25
    assert PS * ES == E and all(c % 32 == 0 for c in CUTS + [HIDDEN])
    NG0 = -(-(E + NB * (GE - 1)) // GE)
    NG = -(-NG0 // 8) * 8
    T1 = NG * KT
    MIN_ROUNDS = -(-(-(-E // GE)) // UNROLL)
    NGD = -(-(-(-E // GE)) // 8) * 8
    GP = NGD // 4
    GLAST = E // GE
    TD = NGD * KT
    W = 128
    ONE, SC = C, C + 1
    FLAT = C * C
    KC = FLAT // P
    RC = 3 * FLAT // 512
    PC = KC // 4
    RING = 4
    K_HIST = 2 * (RC // 3)
    HISTS = (TD - 8) // (2 * RC - K_HIST) // 8 * 8
    AB = 2 * NB + 2

    with ExitStack() as ctx:
        def sb(name, shape, dt=F32):
            return ctx.enter_context(nc.sbuf_tensor(name, shape, dt))

        def sem(name):
            return ctx.enter_context(nc.semaphore(name))

        rec_d = nc.dram_tensor("rec_d", (P * T1, 4), I32).ap()
        tab_d = [nc.dram_tensor(f"tab{h}_d", (N, W), F32).ap() for h in range(2)]
        y_d = nc.dram_tensor("y_d", (N, C), F32).ap()
        gate_d = nc.dram_tensor("gate_d", (2 * RC, 512), F32).ap()

        iota_f = sb("iota_f", [P, 512])
        iota_b = sb("iota_b", [P, 256], BF16)
        ident_f = sb("ident_f", [P, P])
        ident_b = sb("ident_b", [P, P], BF16)
        x0 = sb("x0", [P, NB, C])
        p12 = sb("p12", [P, 2 * R])
        group_block = sb("group_block", [P, BLOCK_LEAD + NG], I32)
        n_extra = sb("n_extra", [P, 1], I32)
        window0 = sb("window0", [P, NGD], I32)
        n_sweeps = sb("n_sweeps", [P, 1], I32)
        rel_dst = sb("rel_dst", [P, NGD, KT])
        src_cols = sb("src_cols", [P, NGD, KT], I32)
        dis = sb("dis", [P, NB])
        weight = sb("weight", [P, C])
        const_rdy = sem("const_rdy")

        rec_e = sb("rec_e", [P, T1, 4], I32)
        rec = rec_e[0:PS, 0:ES, :]
        row = sb("row", [PS, ES], I32)
        stage_row = sb("stage_row", [PS, 2, 16], I32)
        stage_rec = sb("stage_rec", [PS, 2, 16, 4], I32)
        tick = sem("tick")
        staged = [sem(f"staged{h}") for h in range(2)]
        scattered = [sem(f"scattered{h}") for h in range(2)]

        def stage_scatter(sp, b, h):
            wait(sp, scattered[h], b * 256)
            t0 = b * 32 + h * 16
            sp.dma_start(stage_row[:, h, :], row[:, ds(t0, 16)]).then_inc(staged[h], 16)
            sp.dma_start(stage_rec[:, h].rearrange("p t f -> p (t f)"),
                         rec[:, ds(t0, 16), :].rearrange("p t f -> p (t f)")).then_inc(staged[h], 16)

        def scatter(pool, b, h):
            wait_pool(pool, tick, staged[h], b * 32 + 32)
            for j in range(16):
                pool.indirect_dma_start(
                    out=rec_d, out_offset=bass.IndirectOffsetOnAxis(ap=stage_row[:, h, j:j + 1], axis=0),
                    in_=stage_rec[:, h, j, :], in_offset=None).then_inc(scattered[h], 16)

        with ExitStack() as ph:
            def sb1(name, shape, dt=F32):
                return ph.enter_context(nc.sbuf_tensor(name, shape, dt))

            def ps1(name, shape, dt=F32):
                return ph.enter_context(nc.psum_tensor(name, shape, dt))

            def sem1(name):
                return ph.enter_context(nc.semaphore(name))

            iota_i = sb1("iota_i", [P, 512], I32)
            part_i = sb1("part_i", [P, 1], I32)
            part_f = sb1("part_f", [P, 1])
            tri = sb1("tri", [P, P])
            ones = sb1("ones", [P, P])
            idx_i = sb1("idx_i", [PS, 3, ES], I32)
            blk_b = sb1("blk_b", [PS, ES], BF16)
            one_b = sb1("one_b", [PS, ES], BF16)
            mask_b = sb1("mask_b", [PS, ES], BF16)
            mask_2 = sb1("mask_2", [PS, 2, max(b - a for a, b in zip(CUTS, CUTS[1:]))], BF16)
            cum = sb1("cum", [PS, 2, mask_2.shape[2]])
            buf_b = sb1("buf_b", [P, max(ES, TD)])
            pos = buf_b[0:PS, 0:ES]
            counts = sb1("counts", [PS, NB])
            junk_b = cum[:].rearrange("p a b -> p (a b)").bitcast(BF16)[:, 0:ES]
            half_off = sb1("half_off", [P, NB])
            sides = sb1("sides", [PS, NB + 1])
            base = sb1("base", [PS, NB])
            tot = sb1("tot", [P, NB])
            n_groups_i = sb1("n_groups_i", [P, NB], I32)
            n_groups = sb1("n_groups", [P, NB])
            end_group = sb1("end_group", [P, NB])
            gb = sb1("gb", [P, NG])
            blank = sb1("blank", [P, 32, 4], I32)
            grp_dst = sb1("grp_dst", [GP, 4, GE], I32)
            grp_src = sb1("grp_src", [GP, 4, GE], I32)
            grp_f = sb1("grp_f", [GP, 4, GE])
            grp_hi = sb1("grp_hi", [GP, 4, GE])
            lowest = sb1("lowest", [GP, 4])
            highest = sb1("highest", [GP, 4])
            span = sb1("span", [GP, 1])
            dst_t = sb1("dst_t", [P, NGD, KT])
            dst_ti = sb1("dst_ti", [P, NGD, KT], I32)
            lo_t, hi_t = sb1("lo_t", [P, TD])[:], buf_b[:, 0:TD]
            win_f = sb1("win_f", [P, NGD])
            sw_f = sb1("sw_f", [P, 1])
            deg = sb1("deg", [P, NB])
            lo_hot = sb1("lo_hot", [P, 8, P], BF16)
            hi_hot = sb1("hi_hot", [P, 8, 64], BF16)
            h_sb = sb1("h_sb", [P, KC])
            ring = sb1("ring", [P, RING, 4, 512])
            gate_row = sb1("gate_row", [1, 2, 512])

            ps_small = ps1("ps_small", [P, 2, 256])
            ps_t = ps1("ps_t", [P, 2, 512])
            ps_gate = ps1("ps_gate", [1, 2, 512])
            ps_deg = ps1("ps_deg", [P, 512])

            iota_rdy, idx_ld, grp_ld, h_ld, x_ld = map(sem1, ("iota_rdy", "idx_ld", "grp_ld", "h_ld", "x_ld"))
            dv, blank_rdy, blank_st, grp_set = map(sem1, ("dv", "blank_rdy", "blank_st", "grp_set"))
            cnt_rdy, pre_rdy, row_rdy, rec_rdy = map(sem1, ("cnt_rdy", "pre_rdy", "row_rdy", "rec_rdy"))
            grp_rdy, tp_rdy, tp_used, lim_rdy, lim_t = map(sem1, ("grp_rdy", "tp_rdy", "tp_used", "lim_rdy", "lim_t"))
            piece_ld = [sem1(f"piece_ld{i}") for i in range(RING)]
            piece_used, gate_cp = sem1("piece_used"), sem1("gate_cp")
            gate_st = [sem1(f"gate_st{i}") for i in range(2)]
            dtick1 = sem1("dtick1")
            blk_rdy, side_rdy = sem1("blk_rdy"), sem1("side_rdy")
            BY_DVE = NB // 10 // 2 * 10
            hot_rdy, hot_used = sem1("hot_rdy"), sem1("hot_used")

            parts = [(a, min(b, HIDDEN), c) for c, (a, b) in enumerate(zip(CUTS, CUTS[1:]))]
            block = ph.enter_context(nc.Block())

            @block.sync
            def _(sp):
                for i, v in enumerate((src, dst, typ)):
                    sp.dma_start(idx_i[:, i, :], v.rearrange("(p t) -> p t", p=PS)).then_inc(idx_ld, 16)
                sp.wait_ge(grp_set, 2)
                for v, t in ((dst, grp_dst), (src, grp_src)):
                    for c in range(4):
                        n = min(GP, GLAST - c * GP)
                        sp.dma_start(t[0:n, c, :], v[c * GP * GE:(c * GP + n) * GE].rearrange("(p e) -> p e", e=GE)
                                     ).then_inc(grp_ld, 16)
                    n = E - GLAST * GE
                    sp.dma_start(t[GLAST - 3 * GP:GLAST - 3 * GP + 1, 3, 0:n],
                                 v[GLAST * GE:E].rearrange("(p e) -> p e", p=1)).then_inc(grp_ld, 16)
                sp.dma_start(h_sb[:], h_col).then_inc(h_ld, 16)
                for start, end, c in parts:
                    sp.wait_ge(row_rdy, c + 1)
                    if c == 0:
                        sp.wait_ge(rec_rdy, 3)
                        for h in range(2):
                            stage_scatter(sp, 0, h)
                    with loop(sp, max(1, start // 32), end // 32) as b:
                        for h in range(2):
                            stage_scatter(sp, b, h)

            @block.gpsimd
            def _(pool):
                pool.iota(iota_i[:], pattern=[[1, 512]], base=0, channel_multiplier=0).then_inc(iota_rdy, 1)
                pool.iota(part_i[:], pattern=[[0, 1]], base=0, channel_multiplier=1).then_inc(iota_rdy, 1)
                pool.memset(grp_dst[:], PAD_DST).then_inc(grp_set, 1)
                pool.memset(grp_src[:], 0).then_inc(grp_set, 1)

                pool.wait_ge(row_rdy, 1)
                pool.wait_ge(rec_rdy, 3)
                pool.wait_ge(blank_st, 16)
                for h in range(2):
                    scatter(pool, 0, h)
                for start, end, c in parts:
                    pool.wait_ge(row_rdy, c + 1)
                    with loop(pool, max(1, start // 32), end // 32) as b:
                        for h in range(2):
                            scatter(pool, b, h)

            @block.scalar
            def _(act):
                act.wait_ge(blank_rdy, 2)
                act.dma_start(rec_d.rearrange("(p t) f -> p t f", p=P).rearrange("p (a b) f -> p a (b f)", b=32),
                              blank[:].rearrange("p b f -> p (b f)").unsqueeze(1).broadcast_to([P, T1 // 32, 128])
                              ).then_inc(blank_st, 16)
                act.wait_ge(x_ld, 1)
                act.dma_start(x0[0:NODES], x.rearrange("(b p) c -> p b c", p=NODES)).then_inc(x_ld, 16)
                act.wait_ge(idx_ld, 48)
                act.activation(rec[:, :, 1], idx_i[:, 1, :], ACT.Copy).then_inc(rec_rdy, 1)
                act.activation(rec[:, :, 2], idx_i[:, 2, :], ACT.Copy).then_inc(rec_rdy, 1)
                act.wait_ge(blk_rdy, 1)
                for b in range(BY_DVE, NB):
                    act.activation(junk_b, blk_b[:], ACT.Sign, bias=half_off[0:PS, b:b + 1],
                                   accum_out=sides[:, b:b + 1]).then_inc(side_rdy, 1)
                    act.wait_ge(side_rdy, b + 1 - BY_DVE)

                def evacuate(k, s):
                    act.wait_ge(piece_used, (k + 1) * PC)
                    act.activation(gate_row[:, s, :], ps_gate[:, s, :], ACT.Copy).then_inc(gate_cp, 1)
                    act.wait_ge(gate_cp, k + 1)
                    act.dma_start(gate_d[ds(k, 1), :], gate_row[:, s, :]).then_inc(gate_st[s], 16)

                def pieces(k, w, n):
                    for pc in range(PC):
                        wait(act, piece_used, k * PC + pc - RING + 1)
                        act.dma_start(ring[:, pc % RING].rearrange("p q c -> p (q c)"),
                                      w[ds(n, 1), pc].rearrange("a p q c -> (a p) (q c)")).then_inc(piece_ld[pc % RING], 16)

                def stream(k, w, n, s):
                    pieces(k, w, n)
                    if isinstance(k, int) and k == 0:
                        return
                    if not isinstance(k, int) or k > 2:
                        act.wait_ge(gate_st[s], (k - 1 - s) * 8)
                    evacuate(k - 1, s)

                for k in range(4):
                    stream(k, w_ih, k, (k - 1) % 2)
                with loop(act, 4, RC - 1, 2) as k:
                    for u in range(2):
                        stream(k + u, w_ih, k + u, (u - 1) % 2)
                with loop(act, 0, RC - 1, 2) as n:
                    for u in range(2):
                        stream(n + (u + RC), w_hh, n + u, (u - 1) % 2)
                act.wait_ge(gate_st[1], (RC - 1) * 16)
                evacuate(2 * RC - 1, 1)
                for s in range(2):
                    act.wait_ge(gate_st[s], RC * 16)
                act.wait_ge(x_ld, 17)

            @block.tensor
            def _(pe):
                pe.wait_ge(const_rdy, 1)
                pe.wait_ge(cnt_rdy, 1)
                pe.matmul(ps_small[0:PS, 0, 0:NB], lhsT=tri[0:PS, 0:PS], rhs=counts[:], start=True, stop=True)
                pe.matmul(ps_small[:, 1, 0:NB], lhsT=ones[0:PS, :], rhs=counts[:], start=True, stop=True
                          ).then_inc(pre_rdy, 1)
                for i in range(2 * 4 * KT):
                    v, c, k = i // (4 * KT), i // KT % 4, i % KT
                    pe.wait_ge(grp_rdy, v + 1)
                    wait(pe, tp_used, i - 1)
                    pe.transpose(ps_t[:, i % 2, 0:GP], grp_f[:, c, k * P:(k + 1) * P] if v == 0 else
                                 grp_hi[:, c, k * P:(k + 1) * P], ident_f[0:GP, 0:GP]).then_inc(tp_rdy, 1)
                pe.wait_ge(h_ld, 16)

                def chunk(k, s, tile=None):
                    for pc in range(PC):
                        pe.wait_ge(piece_ld[pc % RING], k * (PC // RING * 16) + (pc // RING + 1) * 16)
                        if pc == 0:
                            wait(pe, gate_cp, k - 1)
                        for q in range(4):
                            kc = pc * 4 + q
                            mm = pe.matmul(ps_gate[:, s, :], lhsT=h_sb[:, kc:kc + 1], rhs=ring[:, pc % RING, q, :],
                                           start=(kc == 0), stop=(kc == KC - 1))
                            if q == 3:
                                mm.then_inc(piece_used, 1)
                            if tile is not None:
                                for j in range(kc * HISTS // KC, (kc + 1) * HISTS // KC):
                                    count(tile + j, j % 8)

                def count(i, j, first=False, last=False):
                    pe.wait_ge(hot_rdy, i + 1)
                    pe.matmul(ps_deg[:, 0:NB], lhsT=lo_hot[:, j, :], rhs=hi_hot[:, j, 0:NB], start=first,
                              stop=last, skip_group_check=True).then_inc(hot_used, 1)

                for s in range(2):
                    chunk(s, s)
                with loop(pe, 2, K_HIST - 1, 2) as k0:
                    for s in range(2):
                        chunk(k0 + s, s)
                pe.wait_ge(lim_rdy, 1)
                for c in range(4):
                    pe.transpose(ps_t[:, 0, c * GP:(c + 1) * GP], lowest[:, c:c + 1].broadcast_to([GP, P]),
                                 ident_f[0:GP, 0:GP])
                pe.transpose(ps_t[:, 1, 0:GP], span[:].broadcast_to([GP, P]), ident_f[0:GP, 0:GP]).then_inc(lim_t, 1)
                for j in range(8):
                    count(j, j, first=(j == 0))
                with loop(pe, K_HIST, 2 * RC - 1, 2) as k0:
                    for s in range(2):
                        chunk(k0 + s, s, (k0 - K_HIST) * HISTS + 8 + s * HISTS)
                done = 8 + (2 * RC - K_HIST) * HISTS
                with loop(pe, done, TD - 15, 8) as t0:
                    for j in range(8):
                        count(t0 + j, j)
                for j in range(8):
                    count(TD - 8 + j, j, last=(j == 7))

            @block.vector
            def _(dve):
                link = Chain(dve, dv, dtick1)

                def block_of(to, nodes):
                    link(dve.tensor_scalar(to, nodes, 2.0 ** 14 / NODES, 64.0, ALU.mult, ALU.add))
                    link(dve.tensor_scalar(to, to, 14, None, ALU.logical_shift_right))
                dve.memset(ones[:], 1.0)
                dve.memset(one_b[:], 1.0)
                dve.memset(pos, 0.0)
                dve.memset(gb[:], 0.0)
                link.mark(dve.memset(blank[:], 0))
                link.sync()
                dve.memset(blank[:, :, 0], PAD_LO).then_inc(blank_rdy, 2)
                dve.memset(x0[:], 0.0).then_inc(x_ld, 1)
                link(dve.memset(rec[:, :, 3], 0))
                dve.wait_ge(iota_rdy, 2)
                dve.tensor_copy(iota_b[:], iota_i[:, 0:256])
                dve.tensor_copy(iota_f[:], iota_i[:])
                link(dve.tensor_copy(part_f[:], part_i[:]))
                link.mark(dve.tensor_scalar(ident_f[:], iota_f[:, 0:P], part_f[:], None, ALU.is_equal))
                link.mark(dve.tensor_scalar(ident_b[:], iota_f[:, 0:P], part_f[:], None, ALU.is_equal))
                link.mark(dve.tensor_scalar(half_off[:], iota_f[:, 0:NB], -1.0, 0.5, ALU.mult, ALU.add))
                link.mark(dve.memset(sides[:, NB:NB + 1], -float(ES)))
                link(dve.tensor_scalar(tri[:], iota_f[:, 0:P], part_f[:], None, ALU.is_gt))
                dve.sem_inc(const_rdy, 1)
                dve.wait_ge(idx_ld, 48)
                block_of(row[:], idx_i[:, 0, :])
                link(dve.tensor_copy(blk_b[:], row[:]))
                dve.sem_inc(blk_rdy, 1)
                dve.scalar_tensor_tensor(out=rec[:, :, 0], in0=row[:], scalar=-float(NODES), in1=idx_i[:, 0, :],
                                         op0=ALU.mult, op1=ALU.add).then_inc(rec_rdy, 1)
                def count(b0, n):
                    for b in range(n):
                        link(dve.scalar_tensor_tensor(
                            out=mask_b[:], in0=blk_b[:], scalar=iota_f[0:PS, ds(b0 + b, 1)], in1=one_b[:],
                            op0=ALU.is_equal, op1=ALU.mult, accum_out=counts[:, ds(b0 + b, 1)]))
                link.loop(BY_DVE, 10, 1, count)
                dve.wait_ge(side_rdy, NB - BY_DVE)
                link(dve.tensor_tensor(counts[:, BY_DVE:NB], sides[:, BY_DVE:NB], sides[:, BY_DVE + 1:NB + 1], ALU.subtract))
                link(dve.tensor_scalar(counts[:, BY_DVE:NB], counts[:, BY_DVE:NB], 0.5, None, ALU.mult))
                dve.sem_inc(cnt_rdy, 1)
                dve.wait_ge(pre_rdy, 1)
                link(dve.tensor_scalar(tot[:], ps_small[:, 1, 0:NB], float(GE - 1), None, ALU.add))
                link(dve.tensor_copy(n_groups_i[:], tot[:]))
                link(dve.tensor_scalar(n_groups_i[:], n_groups_i[:], 9, None, ALU.logical_shift_right))
                link(dve.tensor_copy(n_groups[:], n_groups_i[:]))
                link(dve.tensor_tensor_scan(end_group[:], ones[:, 0:NB], n_groups[:], 0.0, ALU.mult, ALU.add))
                link(dve.tensor_tensor(base[:], end_group[0:PS], n_groups[0:PS], ALU.subtract))
                link(dve.scalar_tensor_tensor(out=base[:], in0=base[:], scalar=float(GE), in1=ps_small[0:PS, 0, 0:NB],
                                              op0=ALU.mult, op1=ALU.add))
                def place(b0, n):
                    def mask(b):
                        link.mark(dve.tensor_scalar(mask_2[:, b % 2, 0:w], blk_b[:, t], iota_f[0:PS, ds(b0 + b, 1)], None,
                                                    ALU.is_equal))

                    def add():
                        link.mark(dve.tensor_tensor(pos[:, t], pos[:, t], cum[:, (b - 1) % 2, 0:w], ALU.add))
                    mask(0)
                    for b in range(n):
                        for_b = base[:, ds(b0 + b, 1)]
                        link.sync()
                        link.mark(dve.tensor_tensor_scan(cum[:, b % 2, 0:w], one_b[:, t], mask_2[:, b % 2, 0:w], for_b,
                                                         ALU.mult, ALU.add))
                        if b:
                            add()
                        if b + 1 < n:
                            mask(b + 1)
                        link.sync()
                        link(dve.tensor_scalar(for_b, cum[:, b % 2, w - 1:w], 1.0, None, ALU.mult))
                        link.mark(dve.tensor_tensor(cum[:, b % 2, 0:w], cum[:, b % 2, 0:w], mask_2[:, b % 2, 0:w], ALU.mult))
                    b = n
                    link.sync()
                    add()
                    link.sync()
                for c, (start, end) in enumerate(zip(CUTS, CUTS[1:])):
                    t, w = slice(start, end), end - start
                    link.loop(NB, 10, 5, place)
                    link(dve.tensor_scalar(row[:, t], pos[:, t], -1.0, None, ALU.add))
                    if c == 0:
                        dve.wait_ge(rec_rdy, 3)
                    link.mark(dve.tensor_scalar(idx_i[:, 0, t], row[:, t], P - 1, None, ALU.bitwise_and))
                    link(dve.tensor_scalar(idx_i[:, 1, t], row[:, t], 7, None, ALU.logical_shift_right))
                    dve.scalar_tensor_tensor(out=row[:, t], in0=idx_i[:, 0, t], scalar=float(T1), in1=idx_i[:, 1, t],
                                             op0=ALU.mult, op1=ALU.add).then_inc(row_rdy, 1)
                    if c == 0:
                        dve.wait_ge(grp_ld, 160)
                        link(dve.tensor_copy(grp_f[:], grp_dst[:]))
                        dve.sem_inc(grp_rdy, 1)
                        link(dve.tensor_copy(grp_hi[:], grp_src[:]))
                        dve.sem_inc(grp_rdy, 1)
                        for i in range(2 * 4 * KT):
                            v, q, k = i // (4 * KT), i // KT % 4, i % KT
                            dve.wait_ge(tp_rdy, i + 1)
                            to = (dst_t, src_cols)[v]
                            dve.tensor_copy(to[:, q * GP:(q + 1) * GP, k], ps_t[:, i % 2, 0:GP]).then_inc(tp_used, 1)
                def group(b0, n):
                    for b in range(n):
                        link(dve.scalar_tensor_tensor(out=gb[:], in0=iota_f[:, 0:NG], scalar=end_group[:, ds(b0 + b, 1)],
                                                      in1=gb[:], op0=ALU.is_ge, op1=ALU.add))
                link.loop(NB, 10, 1, group)
                link.mark(dve.memset(group_block[:, 0:BLOCK_LEAD], 0))
                link(dve.tensor_scalar(group_block[:, BLOCK_LEAD:], gb[:], float(NB - 1), None, ALU.min))
                link(dve.tensor_scalar(sw_f[:], end_group[:, NB - 1:NB], float(UNROLL - 1), None, ALU.add))
                link(dve.tensor_copy(n_extra[:], sw_f[:]))
                link(dve.tensor_scalar(n_extra[:], n_extra[:], 3, None, ALU.logical_shift_right))
                link(dve.tensor_copy(sw_f[:], n_extra[:]))
                link(dve.tensor_scalar(n_extra[:], sw_f[:], -float(MIN_ROUNDS), None, ALU.add))
                block_of(grp_dst[:], grp_dst[:])
                link(dve.tensor_copy(grp_hi[:], grp_dst[:]))
                link(dve.tensor_reduce(lowest[:], grp_hi[:], AX, ALU.min))
                link(dve.scalar_tensor_tensor(out=grp_f[:], in0=grp_hi[:], scalar=float(NB), in1=grp_hi[:],
                                              op0=ALU.is_lt, op1=ALU.mult))
                link(dve.tensor_reduce(highest[:], grp_f[:], AX, ALU.max))
                link(dve.tensor_scalar(lowest[:], lowest[:], float(NB - 1), None, ALU.min))
                link(dve.tensor_tensor(highest[:], highest[:], lowest[:], ALU.subtract))
                link(dve.tensor_reduce(span[:], highest[:], AX, ALU.max))
                dve.sem_inc(lim_rdy, 1)
                block_of(dst_ti[:], dst_t[:])
                link(dve.tensor_copy(hi_t, dst_ti[:].rearrange("p g k -> p (g k)")))
                link(dve.scalar_tensor_tensor(out=lo_t, in0=hi_t, scalar=-float(NODES),
                                              in1=dst_t[:].rearrange("p g k -> p (g k)"), op0=ALU.mult, op1=ALU.add))

                def hots(t, j):
                    wait(dve, hot_used, t - 7)
                    dve.tensor_scalar(lo_hot[:, j, :], iota_b[:, 0:P], lo_t[:, ds(t, 1)], None, ALU.is_equal)
                    dve.tensor_scalar(hi_hot[:, j, :], iota_b[:, 0:64], hi_t[:, ds(t, 1)], None, ALU.is_equal
                                      ).then_inc(hot_rdy, 1)
                for j in range(8):
                    hots(j, j)
                with loop(dve, 8, TD - 7, 8) as t0:
                    for j in range(8):
                        hots(t0 + j, j)
                dve.wait_ge(lim_t, 1)
                link.mark(dve.tensor_copy(win_f[:], ps_t[:, 0, 0:NGD]))
                link.mark(dve.tensor_copy(window0[:], ps_t[:, 0, 0:NGD]))
                link(dve.tensor_reduce(sw_f[:], ps_t[:, 1, 0:GP], AX, ALU.max))
                link(dve.tensor_copy(n_sweeps[:], sw_f[:]))
                link(dve.tensor_scalar(n_sweeps[:], n_sweeps[:], 1, None, ALU.logical_shift_right))
                link(dve.tensor_copy(sw_f[:], n_sweeps[:]))
                link(dve.tensor_scalar(n_sweeps[:], sw_f[:], 1.0, None, ALU.add))
                link(dve.scalar_tensor_tensor(out=rel_dst[:], in0=win_f[:].unsqueeze(2).broadcast_to([P, NGD, KT]),
                                              scalar=-float(NODES), in1=dst_t[:], op0=ALU.mult, op1=ALU.add))
                dve.wait_ge(hot_used, TD)
                link(dve.tensor_scalar(deg[:], ps_deg[:, 0:NB], 1.0, None, ALU.add))
                link(dve.tensor_copy(dis[:], deg[:]))

        tab = sb("tab", [P, NB, W])
        lo_e = sb("lo_e", [P, T1])
        typ_e = sb("typ_e", [P, T1])
        dst_e = sb("dst_e", [P, T1], I32)
        acc = sb("acc", [P, NB, C + 1])
        m_run = sb("m_run", [P, NB])
        inv = sb("inv", [P, NB])
        a_split = sb("a_split", [P, NB, 3, R], BF16)
        cuts4 = [(b, min(b + 4, NB)) for b in range(0, NB, 4)]
        half_cut = cuts4[len(cuts4) // 2][0]

        class Project:

            def __init__(self, ph, tag, src, rhs, k, cols, ready):
                self.src, self.rhs, self.k, self.cols, self.ready = src, rhs, k, cols, ready
                self.turned = ph.enter_context(nc.sbuf_tensor(f"turned_{tag}", [P, 2, 4, P], F32))
                self.ps_e = ph.enter_context(nc.psum_tensor(f"ps_e_{tag}", [P, 2, 4, P], F32))
                self.ps_a = ph.enter_context(nc.psum_tensor(f"ps_a_{tag}", [P, 2, 4, P], F32))
                self.turned_rdy, self.copied, self.made, self.taken = (
                    ph.enter_context(nc.semaphore(f"{n}_{tag}")) for n in ("turned_rdy", "copied", "made", "taken"))

            def tensor(self, pe):
                def product(i, lo, hi):
                    pe.wait_ge(self.copied, i + 1)
                    wait(pe, self.taken, i - 1)
                    for b in range(lo, hi):
                        mm = pe.matmul(self.ps_a[:, i % 2, b - lo, 0:self.cols], lhsT=self.turned[0:self.k, i % 2, b - lo, :],
                                       rhs=self.rhs[0:self.k, 0:self.cols], start=True, stop=True)
                    mm.then_inc(self.made, 1)

                for i, (lo, hi) in enumerate(cuts4):
                    pe.wait_ge(self.ready, 1 if hi <= half_cut else 2)
                    wait(pe, self.copied, i - 1)
                    for b in range(lo, hi):
                        mm = pe.transpose(self.ps_e[0:self.k, i % 2, b - lo, :], self.src[:, b, 0:self.k], ident_f[:])
                    mm.then_inc(self.turned_rdy, 1)
                    if i:
                        product(i - 1, *cuts4[i - 1])
                product(len(cuts4) - 1, *cuts4[-1])

            def scalar(self, act, take=None, then={}):
                for i, (lo, hi) in enumerate(cuts4):
                    if i in then:
                        then[i]()
                    act.wait_ge(self.turned_rdy, i + 1)
                    wait(act, self.made, i - 1)
                    act.activation(self.turned[0:self.k, i % 2, 0:hi - lo, :], self.ps_e[0:self.k, i % 2, 0:hi - lo, :],
                                   ACT.Copy).then_inc(self.copied, 1)
                    if take and i:
                        self.take(act, take, i - 1)
                if take:
                    self.take(act, take, len(cuts4) - 1)

            def take(self, eng, take, i):
                lo, hi = cuts4[i]
                eng.wait_ge(self.made, i + 1)
                take(lo, hi, self.ps_a[:, i % 2, 0:hi - lo, 0:self.cols]).then_inc(self.taken, 1)

        class Tables:

            def __init__(self, ph, hop, rows_rdy):
                self.hop = hop
                self.a_all = ph.enter_context(nc.sbuf_tensor(f"a_all_{hop}", [P, NB, 2 * R], F32))
                self.project = Project(ph, hop, tab, p12, P, 2 * R, rows_rdy)
                self.tab_rdy, self.tab_st = (ph.enter_context(nc.semaphore(f"{n}_{hop}")) for n in ("tab_rdy", "tab_st"))

            def tensor(self, pe):
                self.project.tensor(pe)

            def scalar(self, act, then={}):
                self.project.scalar(act, lambda lo, hi, ps: act.activation(self.a_all[:, lo:hi, :], ps, ACT.Copy), then)

            def vector(self, dve, link):
                for half, (lo, hi) in enumerate(((0, half_cut), (half_cut, NB))):
                    dve.wait_ge(self.project.taken, len(cuts4) // 2 if half == 0 else len(cuts4))
                    a = self.a_all[:, lo:hi, 0:R]
                    dve.tensor_copy(tab[:, lo:hi, SC:SC + R], self.a_all[:, lo:hi, R:2 * R]).then_inc(self.tab_rdy, 1)
                    for j in range(3):
                        link(dve.tensor_copy(a_split[:, lo:hi, j, :], a))
                        if j < 2:
                            link(dve.tensor_tensor(a, a, a_split[:, lo:hi, j, :], ALU.subtract))

            def sync(self, sp):
                for half, (lo, hi) in enumerate(((0, half_cut), (half_cut, NB))):
                    sp.wait_ge(self.tab_rdy, half + 1)
                    sp.dma_start(tab_d[self.hop][lo * NODES:hi * NODES].rearrange("(b p) w -> p b w", p=NODES),
                                 tab[0:NODES, lo:hi, :]
                                 ).then_inc(self.tab_st, 16)
                sp.wait_ge(self.tab_st, 32)

        with ExitStack() as ph:
            def sb2(name, shape, dt=F32):
                return ph.enter_context(nc.sbuf_tensor(name, shape, dt))

            def sem2(name):
                return ph.enter_context(nc.semaphore(name))

            g_sb = sb2("g_sb", [C, 2, 3, C])
            b_sb = sb2("b_sb", [C, 2, 3, C])
            h0 = sb2("h0", [C, C])
            rz = sb2("rz", [C, 2, C])
            nn = sb2("nn", [C, C])
            tmp = sb2("tmp", [C, C])
            fcw = sb2("fcw", [C, 2 * C])
            fcb = sb2("fcb", [C, 1])
            rel = sb2("rel", [C, R])
            ps_p = ph.enter_context(nc.psum_tensor("ps_p", [P, 3, 128], F32))
            rows_rdy = sem2("rows_rdy")
            tables = Tables(ph, 0, rows_rdy)
            ld2, fc_ld, dv2, s_rdy, rz_rdy, n_rdy, t_rdy, p_rdy, sq_rdy = map(
                sem2, ("ld2", "fc_ld", "dv2", "s_rdy", "rz_rdy", "n_rdy", "t_rdy", "p_rdy", "sq_rdy"))
            block = ph.enter_context(nc.Block())

            @block.sync
            def _(sp):
                with loop(sp, HIDDEN // 32, ES // 32) as b:
                    for h in range(2):
                        stage_scatter(sp, b, h)

            @block.gpsimd
            def _(pool):
                with loop(pool, HIDDEN // 32, ES // 32) as b:
                    for h in range(2):
                        scatter(pool, b, h)
                for h in range(2):
                    pool.wait_ge(scattered[h], ES // 32 * 256)

            @block.tensor
            def _(pe):
                pe.wait_ge(fc_ld, 48)
                pe.matmul(ps_p[0:C, 0, 0:R], lhsT=fcw[:, 0:C], rhs=rel[:], start=True, stop=True)
                pe.matmul(ps_p[0:C, 1, 0:R], lhsT=fcw[:, C:2 * C], rhs=rel[:], start=True, stop=True)
                pe.matmul(ps_p[C:C + 1, 2, 0:R], lhsT=fcb[:], rhs=rel[:], start=True, stop=True).then_inc(p_rdy, 1)
                tables.tensor(pe)

            @block.vector
            def _(dve):
                link = Chain(dve, dv2)
                link(dve.memset(tab[:], 0.0))
                link(dve.tensor_copy(tab[:, :, 0:C], x0[:]))
                link(dve.memset(tab[:, :, ONE:ONE + 1], 1.0))
                dve.memset(acc[:], 0.0)
                dve.memset(m_run[:], NO_SCORE)
                dve.wait_ge(p_rdy, 1)
                link(dve.memset(p12[:], 0.0))
                link.mark(dve.tensor_copy(p12[0:C, 0:R], ps_p[0:C, 0, 0:R]))
                link.mark(dve.tensor_copy(p12[0:C, R:2 * R], ps_p[0:C, 1, 0:R]))
                link.mark(dve.tensor_copy(p12[C:C + 1, R:2 * R], ps_p[C:C + 1, 2, 0:R]))
                link.sync()
                dve.sem_inc(rows_rdy, 2)
                dve.wait_ge(sq_rdy, 1)
                link(dve.reciprocal(dis[:], dis[:]))
                dve.wait_ge(ld2, 9 * 16)
                link(dve.tensor_tensor(g_sb[:], g_sb[:], b_sb[:], ALU.add))
                dve.tensor_tensor(rz[:], g_sb[:, 0, 0:2, :], g_sb[:, 1, 0:2, :], ALU.add).then_inc(s_rdy, 1)
                dve.wait_ge(rz_rdy, 1)
                link(dve.tensor_tensor(nn[:], rz[:, 0, :], g_sb[:, 1, 2, :], ALU.mult))
                dve.tensor_tensor(nn[:], nn[:], g_sb[:, 0, 2, :], ALU.add).then_inc(n_rdy, 1)
                dve.wait_ge(t_rdy, 1)
                link(dve.tensor_tensor(tmp[:], h0[:], nn[:], ALU.subtract))
                link(dve.tensor_tensor(tmp[:], tmp[:], rz[:, 1, :], ALU.mult))
                link(dve.memset(weight[:], 0.0))
                link(dve.tensor_tensor(weight[0:C, :], tmp[:], nn[:], ALU.add))
                tables.vector(dve, link)

            @block.scalar
            def _(act):
                act.dma_start(fcw[:], fc_w).then_inc(fc_ld, 16)
                act.dma_start(fcb[:], fc_b).then_inc(fc_ld, 16)
                act.dma_start(rel[:], relT).then_inc(fc_ld, 16)
                gv = gate_d.rearrange("(m k) c -> m (k c)", m=2).rearrange("m (t i o) -> m t i o", t=3, o=C)
                for m, b in enumerate((b_ih, b_hh)):
                    for t in range(3):
                        act.dma_start(g_sb[:, m, t, :], gv[m, t]).then_inc(ld2, 16)
                    act.dma_start(b_sb[:, m], b.rearrange("(t i o) -> i t o", t=3, o=C)).then_inc(ld2, 16)
                act.dma_start(h0[:], h_mat).then_inc(ld2, 16)
                act.activation(dis[:], dis[:], ACT.Sqrt).then_inc(sq_rdy, 1)
                act.wait_ge(s_rdy, 1)
                act.activation(rz[:], rz[:], ACT.Sigmoid).then_inc(rz_rdy, 1)
                act.wait_ge(n_rdy, 1)
                act.activation(nn[:], nn[:], ACT.Tanh).then_inc(t_rdy, 1)
                tables.scalar(act)
                tables.sync(act)

        with ExitStack() as ph:
            rec_ld = ph.enter_context(nc.semaphore("rec_ld"))
            block = ph.enter_context(nc.Block())

            @block.sync
            def _(sp):
                sp.dma_start(rec_e[:].rearrange("p t f -> p (t f)"), rec_d.rearrange("(p t) f -> p (t f)", p=P)
                             ).then_inc(rec_ld, 16)

            @block.vector
            def _(dve):
                dve.wait_ge(rec_ld, 16)
                dve.tensor_copy(dst_e[:], rec_e[:, :, 1])
                dve.tensor_copy(lo_e[:], rec_e[:, :, 0])

            @block.scalar
            def _(act):
                act.wait_ge(rec_ld, 16)
                act.activation(typ_e[:], rec_e[:, :, 2], ACT.Copy)

        norm_sq, norm_rdy = sem("norm_sq"), sem("norm_rdy")
        halves = ((0, half_cut), (half_cut, NB))

        def finish(dve, step, n, lo, hi):
            def wide(v):
                return v[:, lo:hi].unsqueeze(2).broadcast_to([P, hi - lo, C])
            emb, sq = tab[:, lo:hi, 0:C], acc[:, lo:hi, 0:C]
            step(dve.tensor_scalar(inv[:, lo:hi], acc[:, lo:hi, C], 0.5, None, ALU.max))
            step(dve.reciprocal(inv[:, lo:hi], inv[:, lo:hi]))
            step(dve.tensor_tensor(sq, sq, wide(inv), ALU.mult))
            step(dve.tensor_tensor(emb, emb, sq, ALU.add))
            step(dve.tensor_tensor(sq, emb, emb, ALU.mult))
            step(dve.tensor_reduce(inv[:, lo:hi], sq, AX, ALU.add))
            dve.tensor_scalar(inv[:, lo:hi], inv[:, lo:hi], 1e-24, None, ALU.max).then_inc(norm_sq, 1)
            dve.wait_ge(norm_rdy, n)
            step(dve.reciprocal(inv[:, lo:hi], inv[:, lo:hi]))
            step(dve.tensor_tensor(emb, emb, wide(inv), ALU.mult))

        def norm_root(act, n, lo, hi):
            act.wait_ge(norm_sq, n)
            act.activation(inv[:, lo:hi], inv[:, lo:hi], ACT.Sqrt).then_inc(norm_rdy, 1)

        for hop in range(2):
            with ExitStack() as ph:
                def sbh(name, shape, dt=F32):
                    return ph.enter_context(nc.sbuf_tensor(f"{name}_{hop}", shape, dt))

                def psh(name, shape, dt=F32):
                    return ph.enter_context(nc.psum_tensor(f"{name}_{hop}", shape, dt))

                def semh(name):
                    return ph.enter_context(nc.semaphore(f"{name}_{hop}"))

                if hop:
                    with ExitStack() as st:
                        rows_rdy, dvt = semh("rows_rdy"), semh("dvt")
                        tables = Tables(st, hop, rows_rdy)
                        with nc.Block() as block:
                            @block.tensor
                            def _(pe):
                                tables.tensor(pe)

                            @block.scalar
                            def _(act):
                                norm_root(act, 1, *halves[0])
                                tables.scalar(act, {3: lambda: norm_root(act, 2, *halves[1])})

                            @block.vector
                            def _(dve):
                                link = Chain(dve, dvt)
                                for n, (lo, hi) in enumerate(halves):
                                    finish(dve, link, n + 1, lo, hi)
                                    dve.sem_inc(rows_rdy, 1)
                                dve.memset(acc[:], 0.0)
                                dve.memset(m_run[:], NO_SCORE)
                                tables.vector(dve, link)

                            @block.sync
                            def _(sp):
                                tables.sync(sp)

                stage_idx = sbh("stage_idx", [P, 2, 16], I32)
                rows = sbh("rows", [P, 8, KT, W])
                hot = sbh("hot", [P, 2, KT, P], BF16)
                hot_t = sbh("hot_t", [P, 2, GE], BF16)
                lower = sbh("lower", [P, 2, GE], BF16)
                picked = sbh("picked", [P, KT, R])
                s_raw = sbh("s_raw", [P, 2, KT])
                score = sbh("score", [P, 2, KT])
                masked = sbh("masked", [P, 2, GE])
                m_group = sbh("m_group", [P, 2])
                m_new = sbh("m_new", [P, 2])
                m_neg = sbh("m_neg", [P, 2])
                m_diff = sbh("m_diff", [P, 2, 2])
                alpha = sbh("alpha", [P, 2, 2])
                prob_t = sbh("prob_t", [P, 2, GE])
                prob = sbh("prob", [P, 2, GE])
                kept = sbh("kept", [P, 2, C + 1])
                ps_hot = psh("ps_hot", [P, 2 * GE], BF16)
                ps_x = psh("ps_x", [P, 2, 512])
                ps_s = psh("ps_s", [P, 2, GE])
                ps_p = psh("ps_p", [P, GE])
                ps_g = psh("ps_g", [P, 2, 512])
                (hot_rdy, hot_turned, hot_t_rdy, lower_rdy, x_rdy, score_rdy, s_spread, masked_rdy, exp_rdy, p_turned,
                 prob_rdy, summed, added, tick, dvh) = map(semh, (
                     "hot_rdy", "hot_turned", "hot_t_rdy", "lower_rdy", "x_rdy", "score_rdy", "s_spread", "masked_rdy",
                     "exp_rdy", "p_turned", "prob_rdy", "summed", "added", "tick", "dvh"))
                dtick = semh("dtick")
                landed = [semh(f"landed{i}") for i in range(8)]
                staged = [semh(f"staged{h}") for h in range(2)]
                def live(eng):
                    return eng.value_load(n_extra[0:1, 0:1], min_val=0, max_val=NG // UNROLL - MIN_ROUNDS) + MIN_ROUNDS

                with nc.Block() as block:
                    @block.sync
                    def _(sp):
                        def half(it, h):
                            for g in range(4):
                                wait(sp, landed[h * 4 + g], it * 64)
                            sp.dma_start(stage_idx[:, h, :], dst_e[:, ds((it * 8 + h * 4) * KT, 16)]).then_inc(staged[h], 16)
                        rounds = live(sp)
                        for h in range(2):
                            half(0, h)
                        with loop(sp, 1, rounds) as it:
                            for h in range(2):
                                half(it, h)

                    @block.gpsimd
                    def _(pool):
                        def half(it, h):
                            g0 = it * 8 + h * 4
                            wait_pool(pool, tick, summed, g0 - 7)
                            wait_pool(pool, tick, staged[h], it * 16 + 16)
                            for g in range(4):
                                if g:
                                    wait_pool(pool, tick, summed, g0 + g - 7)
                                for k in range(KT):
                                    j = g * KT + k
                                    pool.indirect_dma_start(
                                        out=rows[:, h * 4 + g, k, :], out_offset=None, in_=tab_d[hop],
                                        in_offset=bass.IndirectOffsetOnAxis(ap=stage_idx[:, h, j:j + 1], axis=0)
                                    ).then_inc(landed[h * 4 + g], 16)
                        pool_n = live(pool)
                        for h in range(2):
                            half(0, h)
                        with loop(pool, 1, pool_n) as it:
                            for h in range(2):
                                half(it, h)

                    @block.tensor
                    def _(pe):
                        def spread(g, p):
                            wait(pe, score_rdy, g + 1)
                            wait(pe, masked_rdy, g - 1)
                            for k in range(KT):
                                mm = pe.transpose(ps_s[:, p, k * P:(k + 1) * P],
                                                  score[:, p, k:k + 1].broadcast_to([P, P]), ident_f[:])
                            mm.then_inc(s_spread, 1)

                        def turn_prob(g, p):
                            wait(pe, exp_rdy, g + 1)
                            wait(pe, prob_rdy, g)
                            for k in range(KT):
                                mm = pe.transpose(ps_p[:, k * P:(k + 1) * P], prob_t[:, p, k * P:(k + 1) * P],
                                                  ident_f[:])
                            mm.then_inc(p_turned, 1)

                        def turn_hot(g, p):
                            wait(pe, hot_rdy, g + 1)
                            wait(pe, lower_rdy, g)
                            for k in range(KT):
                                mm = pe.transpose(ps_hot[:, k * P:(k + 1) * P], hot[:, p, k, :], ident_b[:])
                            mm.then_inc(hot_turned, 1)

                        def scores(g, p, u, bb):
                            wait(pe, landed[u], (g - u) * 8 + 64)
                            wait(pe, hot_t_rdy, g + 1)
                            wait(pe, score_rdy, g - 1)
                            for k in range(KT):
                                for j in range(3):
                                    pe.matmul(ps_x[:, p, k * R:(k + 1) * R], lhsT=hot_t[:, p, k * P:(k + 1) * P],
                                              rhs=a_split[:, ds(bb, 1), j, :].rearrange("p a r -> p (a r)"),
                                              start=(k == 0 and j == 0), stop=False, skip_group_check=True)
                            mm = pe.matmul(ps_x[:, p, 0:KT * R], lhsT=ident_f[:], rhs=rows[:, u, :, SC:SC + R],
                                           start=False, stop=True, skip_group_check=True)
                            mm.then_inc(x_rdy, 1)

                        def sums(g, p, u):
                            wait(pe, prob_rdy, g + 1)
                            wait(pe, added, g - 1)
                            for k in range(KT):
                                mm = pe.matmul(ps_g[:, p, 0:C + 1], lhsT=prob[:, p, k * P:(k + 1) * P],
                                               rhs=rows[:, u, k, 0:C + 1], start=(k == 0), stop=(k == KT - 1))
                            mm.then_inc(summed, 1)

                        def body(i, u, stages, block_of):
                            _, a, b, c = stages
                            if a:
                                turn_hot(i - 1, (u - 1) % 2)
                            if b:
                                spread(i - 2, u % 2)
                            if c:
                                turn_prob(i - 3, (u - 3) % 2)
                            if a:
                                scores(i - 1, (u - 1) % 2, (u - 1) % 8, block_of(1))
                            if c:
                                sums(i - 3, (u - 3) % 2, (u - 3) % 8)
                        pipelined(pe, live(pe) * UNROLL, body, group_block, NB - 1)

                    @block.scalar
                    def _(act):
                        def body(i, u, stages, _):
                            _, a, b, c = stages
                            p = (u - 1) % 2
                            if a:
                                g = i - 1
                                wait(act, hot_turned, g + 1)
                                wait(act, x_rdy, g - 1)
                                act.activation(hot_t[:, p, :], ps_hot[:, 0:GE], ACT.Copy).then_inc(hot_t_rdy, 1)
                                wait(act, masked_rdy, g - 1)
                                act.activation(lower[:, p, :], ps_hot[:, 0:GE], ACT.Copy, bias=-BIG, scale=BIG
                                               ).then_inc(lower_rdy, 1)
                            if c:
                                g = i - 3
                                wait(act, p_turned, g + 1)
                                wait(act, summed, g - 1)
                                act.activation(prob[:, p, :], ps_p[:], ACT.Copy).then_inc(prob_rdy, 1)
                            if b:
                                g, q = i - 2, 1 - p
                                wait(act, masked_rdy, g + 1)
                                wait(act, p_turned, g - 1)
                                act.activation(prob_t[:, q, :], masked[:, q, :], ACT.Exp, bias=m_neg[:, q:q + 1])
                                wait(act, added, g - 1)
                                act.activation(alpha[:, q, :], m_diff[:, q, :], ACT.Exp).then_inc(exp_rdy, 1)
                        pipelined(act, live(act) * UNROLL, body)

                    @block.vector
                    def _(dve):
                        link = Chain(dve, dvh)

                        def body(i, u, stages, block_of):
                            z, a, b, c = stages
                            if b:
                                g, p = i - 2, u % 2
                                bb = block_of(2)
                                wait(dve, lower_rdy, g + 1)
                                wait(dve, exp_rdy, g - 1)
                                wait(dve, s_spread, g + 1)
                                dve.sem_inc(dtick, 1)
                                link.mark(dve.tensor_tensor_reduce(masked[:, p, :], lower[:, p, :], ps_s[:, p, :], 1.0,
                                                                   -3e38, ALU.add, ALU.max, m_group[:, p:p + 1]))

                            def one_hot(k, last=False):
                                if z:
                                    ins = dve.tensor_scalar(hot[:, u % 2, k, :], iota_b[:, 0:P],
                                                            lo_e[:, ds(i * KT + k, 1)], None, ALU.is_equal)
                                    if last:
                                        ins.then_inc(hot_rdy, 1)
                            if z:
                                wait(dve, hot_turned, i - 1)
                            one_hot(0)
                            one_hot(1)
                            if b:
                                link.sync()
                                link.mark(dve.tensor_tensor(m_new[:, p:p + 1], m_run[:, ds(bb, 1)], m_group[:, p:p + 1],
                                                            ALU.max))
                            one_hot(2)
                            if b:
                                link.sync()
                                dve.tensor_tensor(m_diff[:, p, 0:1], m_run[:, ds(bb, 1)], m_new[:, p:p + 1], ALU.subtract)
                                dve.tensor_tensor(m_diff[:, p, 1:2], m_group[:, p:p + 1], m_new[:, p:p + 1], ALU.subtract)
                                dve.tensor_scalar(m_neg[:, p:p + 1], m_group[:, p:p + 1], -1.0, None, ALU.mult
                                                  ).then_inc(masked_rdy, 1)
                            one_hot(3, last=True)
                            if b:
                                wait(dve, masked_rdy, g + 1)
                                link.mark(dve.tensor_scalar(m_run[:, ds(bb, 1)], m_new[:, p:p + 1], 1.0, None, ALU.mult))
                            if a:
                                g, q = i - 1, (u - 1) % 2
                                wait(dve, x_rdy, g + 1)
                                for k in range(KT):
                                    ins = dve.scalar_tensor_tensor(
                                        out=picked[:, k, :], in0=iota_f[:, 0:R], scalar=typ_e[:, ds(g * KT + k, 1)],
                                        in1=ps_x[:, q, k * R:(k + 1) * R], op0=ALU.is_equal, op1=ALU.mult,
                                        accum_out=s_raw[:, q, k:k + 1])
                                    link.mark(ins)
                                wait(dve, s_spread, g - 1)
                                link.sync()
                                dve.scalar_tensor_tensor(out=score[:, q, :], in0=s_raw[:, q, :], scalar=0.2,
                                                         in1=s_raw[:, q, :], op0=ALU.mult, op1=ALU.max
                                                         ).then_inc(score_rdy, 1)
                            if c:
                                g, q = i - 3, (u - 3) % 2
                                sums_of = acc[:, ds(block_of(3), 1), :].rearrange("p a c -> p (a c)")
                                wait(dve, summed, g + 1)
                                wait(dve, added, g)
                                link(dve.tensor_scalar(kept[:, q, :], sums_of, alpha[:, q, 0:1], None, ALU.mult))
                                dve.scalar_tensor_tensor(out=sums_of, in0=ps_g[:, q, 0:C + 1], scalar=alpha[:, q, 1:2],
                                                         in1=kept[:, q, :], op0=ALU.mult, op1=ALU.add
                                                         ).then_inc(added, 1)
                        n = live(dve) * UNROLL
                        pipelined(dve, n, body, group_block, NB - 1, link)
                        dve.wait_ge(added, n)
                        dve.sem_inc(dtick, 1)

        with ExitStack() as ph:
            def sbl(name, shape, dt=F32):
                return ph.enter_context(nc.sbuf_tensor(name, shape, dt))

            def psl(name, shape, dt=F32):
                return ph.enter_context(nc.psum_tensor(name, shape, dt))

            def seml(name):
                return ph.enter_context(nc.semaphore(name))

            y = sbl("y", [P, NB, C])
            total = sbl("total", [P, AB, C])
            cen = acc[:, :, 0:C]
            ssq = tab[:, :, 0:C]
            mean = sbl("mean", [P, NB])
            var = sbl("var", [P, NB])
            rows = sbl("y_rows", [P, 4, KT, C])
            stage_idx = sbl("stage_src", [P, 2, 16], I32)
            near = sbl("near", [P, 2, KT, 2 * NODES])
            var_rdy, sd_rdy = seml("var_rdy"), seml("sd_rdy")

            def layernorm(dve, link, n, lo=0, hi=NB):
                def wide(v):
                    return v[:, lo:hi].unsqueeze(2).broadcast_to([P, hi - lo, C])
                link(dve.tensor_reduce(mean[:, lo:hi], x0[:, lo:hi], AX, ALU.add))
                link(dve.tensor_scalar(mean[:, lo:hi], mean[:, lo:hi], 1.0 / C, None, ALU.mult))
                link(dve.tensor_tensor(cen[:, lo:hi], x0[:, lo:hi], wide(mean), ALU.subtract))
                link(dve.tensor_tensor(ssq[:, lo:hi], cen[:, lo:hi], cen[:, lo:hi], ALU.mult))
                link(dve.tensor_reduce(var[:, lo:hi], ssq[:, lo:hi], AX, ALU.add))
                dve.tensor_scalar(var[:, lo:hi], var[:, lo:hi], 1.0 / C, 1e-5, ALU.mult, ALU.add).then_inc(var_rdy, 1)
                dve.wait_ge(sd_rdy, n)
                link(dve.reciprocal(var[:, lo:hi], var[:, lo:hi]))
                link(dve.tensor_tensor(x0[:, lo:hi], cen[:, lo:hi], wide(var), ALU.mult))

            def root(act, n, lo=0, hi=NB):
                act.wait_ge(var_rdy, n)
                act.activation(var[:, lo:hi], var[:, lo:hi], ACT.Sqrt).then_inc(sd_rdy, 1)

            with ExitStack() as st:
                x_rdy, y_rdy, y_st, dvy = map(seml, ("x_rdy", "y_rdy", "y_st", "dvy"))
                times_w = Project(st, "y", x0, weight, C, C, x_rdy)
                with nc.Block() as block:
                    @block.vector
                    def _(dve):
                        link = Chain(dve, dvy)
                        left = iter(range(len(cuts4)))

                        def take_next():
                            i = next(left, None)
                            if i is not None:
                                times_w.take(dve, lambda lo, hi, ps: dve.tensor_tensor(
                                    y[:, lo:hi, :], ps, dis[:, lo:hi].unsqueeze(2).broadcast_to([P, hi - lo, C]), ALU.mult), i)

                        def weave(takes):
                            spare = iter(range(takes))

                            def step(ins):
                                link(ins)
                                if next(spare, None) is not None:
                                    take_next()
                            return step
                        for n, (lo, hi) in enumerate(halves):
                            finish(dve, weave(2) if n else link, 3 + n, lo, hi)
                            step = weave(len(cuts4) // 2 - 3) if n else link
                            step(dve.tensor_tensor(x0[:, lo:hi], x0[:, lo:hi], tab[:, lo:hi, 0:C], ALU.add))
                            layernorm(dve, step, n + 1, lo, hi)
                            dve.sem_inc(x_rdy, 1)
                        for i in cuts4:
                            take_next()
                        dve.memset(total[:], 0.0)

                    @block.scalar
                    def _(act):
                        norm_root(act, 3, *halves[0])
                        root(act, 1, *halves[0])
                        times_w.scalar(act, then={2: lambda: norm_root(act, 4, *halves[1]),
                                                  len(cuts4) // 2: lambda: root(act, 2, *halves[1])})

                    @block.tensor
                    def _(pe):
                        times_w.tensor(pe)

                    @block.sync
                    def _(sp):
                        for half, (lo, hi) in enumerate(halves):
                            sp.wait_ge(times_w.taken, len(cuts4) // 2 if half == 0 else len(cuts4))
                            sp.dma_start(y_d[lo * NODES:hi * NODES].rearrange("(b p) w -> p b w", p=NODES), y[0:NODES, lo:hi, :]
                                         ).then_inc(y_st, 16)
                        sp.wait_ge(y_st, 32)

            ps_g = psl("ps_gy", [P, 2, 512])
            near_rdy, summed, added, tick, dvl, fin_rdy, out_st = map(seml, (
                "near_rdy", "summed_y", "added_y", "tick_y", "dvl", "fin_rdy", "out_st"))
            staged = [seml(f"staged_y{h}") for h in range(2)]
            landed = [seml(f"landed_y{i}") for i in range(4)]
            dtick_l = seml("dtick_l")
            AHEAD = 5
            with nc.Block() as block:
                @block.sync
                def _(sp):
                    sweeps = sp.value_load(n_sweeps[0:1, 0:1], min_val=1, max_val=NB // 2 + 1)

                    with loop(sp, 0, sweeps) as w:
                        with loop(sp, 0, NGD // 8) as it:
                            for h in range(2):
                                sp.wait_ge(summed, w * NGD + it * 8 + (h * 4 - 4 + AHEAD))
                                sp.dma_start(stage_idx[:, h, :], src_cols[:, ds(it * 8 + h * 4, 4), :]
                                             .rearrange("p g k -> p (g k)")).then_inc(staged[h], 16)
                    for n, (lo, hi) in enumerate(halves):
                        sp.wait_ge(fin_rdy, n + 1)
                        sp.dma_start(out[lo * NODES:hi * NODES].rearrange("(b p) c -> p b c", p=NODES),
                                     x0[0:NODES, lo:hi, :]).then_inc(out_st, 16)
                    sp.wait_ge(out_st, 32)

                @block.gpsimd
                def _(pool):
                    sweeps = pool.value_load(n_sweeps[0:1, 0:1], min_val=1, max_val=NB // 2 + 1)
                    with loop(pool, 0, sweeps) as w:
                        with loop(pool, 0, NGD // 8) as it:
                            for h in range(2):
                                f0 = w * NGD + it * 8 + h * 4
                                wait_pool(pool, tick, summed, f0 - 3 + AHEAD)
                                wait_pool(pool, tick, staged[h], (w * (NGD // 8) + it) * 16 + 16)
                                for g in range(4):
                                    if g:
                                        wait_pool(pool, tick, summed, f0 + g - 3 + AHEAD)
                                    for k in range(KT):
                                        j = g * KT + k
                                        pool.indirect_dma_start(
                                            out=rows[:, g, k, :], out_offset=None, in_=y_d,
                                            in_offset=bass.IndirectOffsetOnAxis(ap=stage_idx[:, h, j:j + 1], axis=0)
                                        ).then_inc(landed[g], 16)

                @block.tensor
                def _(pe):
                    pe.sem_inc(summed, AHEAD)
                    sweeps = pe.value_load(n_sweeps[0:1, 0:1], min_val=1, max_val=NB // 2 + 1)
                    with loop(pe, 0, sweeps) as w:
                        with loop(pe, 0, NGD - 3, 4) as i0:
                            for u in range(4):
                                f = w * NGD + i0 + u
                                pe.wait_ge(landed[u], (w * NGD + i0) * 16 + 64)
                                pe.wait_ge(near_rdy, f + 1)
                                pe.wait_ge(added, f - 1 + AHEAD)
                                for j in range(2):
                                    for k in range(KT):
                                        mm = pe.matmul(ps_g[0:NODES, u % 2, j * C:(j + 1) * C],
                                                       lhsT=near[:, u % 2, k, j * NODES:(j + 1) * NODES],
                                                       rhs=rows[:, u, k, :], start=(k == 0), stop=(k == KT - 1))
                                mm.then_inc(summed, 1)

                @block.vector
                def _(dve):
                    link = Chain(dve, dvl)
                    dve.sem_inc(added, AHEAD)
                    sweeps = dve.value_load(n_sweeps[0:1, 0:1], min_val=1, max_val=NB // 2 + 1)

                    def windows(i, f, u):
                        dve.wait_ge(summed, f - 1 + AHEAD)
                        for k in range(KT):
                            ins = dve.tensor_scalar(near[:, u % 2, k, :], iota_f[:, 0:2 * NODES], rel_dst[:, ds(i, 1), k],
                                                    None, ALU.is_equal)
                        ins.then_inc(near_rdy, 1)

                    def add(i, f, w, u):
                        first = dve.value_load(window0[0:1, ds(i, 1)], min_val=0, max_val=NB - 1)
                        t = total[0:NODES, ds(first + w * 2, 2), :]
                        dve.wait_ge(summed, f + 1 + AHEAD)
                        dve.wait_ge(added, f + AHEAD)
                        dve.tensor_tensor(t, t, ps_g[0:NODES, u % 2, 0:2 * C].rearrange("p (j c) -> p j c", j=2), ALU.add).then_inc(added, 1)

                    with loop(dve, 0, sweeps) as w:
                        f0 = w * NGD
                        windows(0, f0, 0)
                        for u in range(1, 4):
                            windows(u, f0 + u, u)
                            add(u - 1, f0 + u - 1, w, u - 1)
                        with loop(dve, 4, NGD - 3, 4) as i0:
                            for u in range(4):
                                windows(i0 + u, f0 + i0 + u, u)
                                add(i0 + u - 1, f0 + i0 + (u - 1), w, u - 1)
                        add(NGD - 1, f0 + NGD - 1, w, 3)
                        dve.tensor_scalar(rel_dst[:], rel_dst[:], -2.0 * NODES, None, ALU.add).then_inc(dvl, 1)
                        dve.wait_ge(dvl, w + 1)
                        dve.sem_inc(dtick_l, 1)

                    link.base = sweeps
                    for n, (lo, hi) in enumerate(halves):
                        v = y[:, lo:hi]
                        link(dve.tensor_tensor(v, v, total[:, lo:hi, :], ALU.add))
                        link(dve.tensor_tensor(v, v, dis[:, lo:hi].unsqueeze(2).broadcast_to([P, hi - lo, C]), ALU.mult))
                        link(dve.scalar_tensor_tensor(out=x0[:, lo:hi], in0=v, scalar=0.0, in1=x0[:, lo:hi],
                                                      op0=ALU.max, op1=ALU.add))
                        layernorm(dve, link, 3 + n, lo, hi)
                        dve.sem_inc(fin_rdy, 1)

                @block.scalar
                def _(act):
                    for n, (lo, hi) in enumerate(halves):
                        root(act, 3 + n, lo, hi)


def kernel(**inputs):
    import numpy as np
    import concourse.bacc as bacc
    from concourse.bass_utils import run_bass_kernel_spmd

    def turned(w):
        r, k = w.shape
        return np.ascontiguousarray(w.reshape(r // 512, 512, k // 512, 4, 128).transpose(0, 2, 4, 3, 1))

    a = {k: np.asarray(v) for k, v in inputs.items()}
    arrays = {
        "x": a["x"], "src": a["src"], "dst": a["dst"], "typ": a["edge_type_50"],
        "relT": np.ascontiguousarray(a["L0_gnn_relation_emb"].T),
        "fc_w": a["L0_gnn_fc_w"], "fc_b": np.ascontiguousarray(a["L0_gnn_fc_b"][:, None]),
        "w_ih": turned(a["L1_gnn_w_ih"]), "w_hh": turned(a["L1_gnn_w_hh"]),
        "h_col": np.ascontiguousarray(a["L1_gnn_initial_weight"].reshape(-1, 128).T),
        "h_mat": a["L1_gnn_initial_weight"],
        "b_ih": a["L1_gnn_b_ih"], "b_hh": a["L1_gnn_b_hh"],
    }
    nc = bacc.Bacc("TRN2", target_bir_lowering=False, num_devices=1)
    args = [nc.dram_tensor(k, v.shape, mybir.dt.from_np(v.dtype), kind="ExternalInput").ap() for k, v in arrays.items()]
    out = nc.dram_tensor("out", a["x"].shape, F32, kind="ExternalOutput").ap()
    gnn_kernel(nc, *args, out)
    r = run_bass_kernel_spmd(nc, [arrays], core_ids=[0])
    return r.results[0]["out"]
```
